# Optimizing a Trainium2 kernel written in Bass

```python
import numpy as np
import jax
import jax.numpy as jnp

def _softmax(x, axis=-1):
    return jax.nn.softmax(x, axis=axis)

def _gelu(x):
    return jax.nn.gelu(x, approximate=True)

def _silu(x):
    return jax.nn.silu(x)

def _sigmoid(x):
    return jax.nn.sigmoid(x)

def _layernorm(x, axis=-1, eps=1e-05):
    m = jnp.mean(x, axis=axis, keepdims=True)
    v = jnp.var(x, axis=axis, keepdims=True)
    return (x - m) / jnp.sqrt(v + eps)

def _scatter_add(tgt, idx, src, axis=0):
    return tgt.at[idx].add(src)

def _segment_sum(src, seg, n):
    return jax.ops.segment_sum(src, seg, n)
kernel_name = 'mk_decoder_preln_d1_seqx_r4_0006bb'

def setup_inputs(seed: int=0):
    np.random.seed(seed)
    _w = jnp.asarray

    def _rec_inputs():
        import jax
        import jax.numpy as jnp
        _rk = jax.random.key(seed)
        x = 7.22e-05 + 1 * jax.random.normal(jax.random.fold_in(_rk, 1), (8, 256, 256), jnp.float32)
        _lenS = 256 - jax.random.randint(jax.random.fold_in(_rk, 7), (8,), 0, max(1, 256 // 4) + 1, jnp.int32)
        _lenS2 = 256 - jax.random.randint(jax.random.fold_in(_rk, 8), (8,), 0, max(1, 256 // 4) + 1, jnp.int32)
        _ctx_1024P = jax.random.normal(jax.random.fold_in(_rk, 11), (8, 16, 256), jnp.float32)
        _ctx_1024c = jax.random.dirichlet(jax.random.fold_in(_rk, 511), 0.3 * jnp.ones((16,), jnp.float32), (8, 256))
        _ctx_1024t = jnp.einsum('bsk,bkd->bsd', _ctx_1024c, _ctx_1024P)
        _ctx_1024t = _ctx_1024t * jax.lax.rsqrt(jnp.mean(jnp.square(_ctx_1024t)) + 1e-12) * 0.953939
        ctx_1024 = 4.13588e-05 + 0.999923 * (_ctx_1024t + 0.3 * jax.random.normal(jax.random.fold_in(_rk, 611), (8, 256, 256), jnp.float32))
        return (x, ctx_1024)
    x, ctx_1024 = _rec_inputs()

    def _L0_attn_setup():
        import jax, jax.numpy as jnp
        import numpy as np
        GAMMA = 0.96875
        H = 256
        B = 4
        L = 512
        key = jax.random.key(seed)
        k0, k1, k2, k3, k4 = jax.random.split(key, 5)
        x = jax.random.normal(k0, (B, L, H), dtype=jnp.float32)
        weight_q = jax.random.normal(k1, (H, H), dtype=jnp.float32) / H
        weight_k = jax.random.normal(k2, (H, H), dtype=jnp.float32) / H
        weight_v = jax.random.normal(k3, (H, H), dtype=jnp.float32) / H
        theta = jax.random.normal(k4, (H,), dtype=jnp.float32) / H
        return {'x': x, 'weight_q': weight_q, 'weight_k': weight_k, 'weight_v': weight_v, 'theta': theta}
    _L0_attn_all = _L0_attn_setup()
    _L0_attn_in = {k: v for k, v in _L0_attn_all.items() if k in ('weight_q', 'weight_k', 'weight_v', 'theta')}
    del _L0_attn_all

    def _L0_xattn_setup():
        import jax, jax.numpy as jnp
        import numpy as np
        INF = 10000000000.0
        D_MODEL = 256
        N_HEADS = 16
        SCALE = float(np.sqrt(D_MODEL))
        key = jax.random.key(seed)
        ks = jax.random.split(key, 8)
        B, S, D = (4, 512, D_MODEL)
        s = 1.0 / np.sqrt(D)
        return {'query': jax.random.normal(ks[0], (B, S, D), jnp.float32), 'key': jax.random.normal(ks[1], (B, S, D), jnp.float32), 'value': jax.random.normal(ks[2], (B, S, D), jnp.float32), 'wq': jax.random.normal(ks[3], (D, D), jnp.float32) * s, 'bq': jnp.zeros((D,), jnp.float32), 'wk': jax.random.normal(ks[4], (D, D), jnp.float32) * s, 'bk': jnp.zeros((D,), jnp.float32), 'wv': jax.random.normal(ks[5], (D, D), jnp.float32) * s, 'bv': jnp.zeros((D,), jnp.float32), 'wo': jax.random.normal(ks[6], (D, D), jnp.float32) * s, 'bo': jnp.zeros((D,), jnp.float32)}
    _L0_xattn_all = _L0_xattn_setup()
    _L0_xattn_in = {k: v for k, v in _L0_xattn_all.items() if k in ('wq', 'bq', 'wk', 'bk', 'wv', 'bv', 'wo', 'bo')}
    del _L0_xattn_all

    def _L0_ffn_setup():
        import jax, jax.numpy as jnp
        import numpy as np
        CAPACITY_FACTOR = 1.25
        key = jax.random.key(seed)
        k1, k2, k3, k4 = jax.random.split(key, 4)
        B, S, D, E, H = (2, 512, 256, 16, 1024)
        inputs = jax.random.normal(k1, (B, S, D), dtype=jnp.float32)
        gate_w = jax.random.normal(k2, (E, D), dtype=jnp.float32) / np.float32(np.sqrt(D))
        w1 = jax.random.normal(k3, (E, D, H), dtype=jnp.float32) / np.float32(np.sqrt(D))
        w2 = jax.random.normal(k4, (E, H, D), dtype=jnp.float32) / np.float32(np.sqrt(H))
        return {'inputs': inputs, 'gate_w': gate_w, 'w1': w1, 'w2': w2}
    _L0_ffn_all = _L0_ffn_setup()
    _L0_ffn_in = {k: v for k, v in _L0_ffn_all.items() if k in ('gate_w', 'w1', 'w2')}
    del _L0_ffn_all
    return {'x': x, 'ctx_1024': ctx_1024, 'L0_attn_weight_q': _L0_attn_in['weight_q'], 'L0_attn_weight_k': _L0_attn_in['weight_k'], 'L0_attn_weight_v': _L0_attn_in['weight_v'], 'L0_attn_theta': _L0_attn_in['theta'], 'L0_xattn_wq': _L0_xattn_in['wq'], 'L0_xattn_bq': _L0_xattn_in['bq'], 'L0_xattn_wk': _L0_xattn_in['wk'], 'L0_xattn_bk': _L0_xattn_in['bk'], 'L0_xattn_wv': _L0_xattn_in['wv'], 'L0_xattn_bv': _L0_xattn_in['bv'], 'L0_xattn_wo': _L0_xattn_in['wo'], 'L0_xattn_bo': _L0_xattn_in['bo'], 'L0_ffn_gate_w': _L0_ffn_in['gate_w'], 'L0_ffn_w1': _L0_ffn_in['w1'], 'L0_ffn_w2': _L0_ffn_in['w2']}

def reference(x, ctx_1024, L0_attn_weight_q, L0_attn_weight_k, L0_attn_weight_v, L0_attn_theta, L0_xattn_wq, L0_xattn_bq, L0_xattn_wk, L0_xattn_bk, L0_xattn_wv, L0_xattn_bv, L0_xattn_wo, L0_xattn_bo, L0_ffn_gate_w, L0_ffn_w1, L0_ffn_w2):
    import jax
    import jax.numpy as jnp

    def _L0_attn_ref(x, weight_q, weight_k, weight_v, theta):
        import jax, jax.numpy as jnp
        import numpy as np
        GAMMA = 0.96875
        H = 256
        B = 4
        L = 512
        Bb, Ll, Hh = x.shape
        dt = x.dtype
        seq = jnp.arange(1, Ll + 1, dtype=dt)
        zero = jnp.asarray(0.0, dtype=dt)
        thetas = jnp.exp(zero * seq[:, None] * theta[None, :])
        theta_conj = thetas
        q = jnp.matmul(x, weight_q) * thetas[None]
        k = jnp.matmul(x, weight_k) * theta_conj[None]
        v = jnp.matmul(x, weight_v)
        n = jnp.arange(Ll)
        diff = n[:, None] - n[None, :]
        D = jnp.where(diff >= 0, jnp.asarray(GAMMA, dt) ** diff.astype(dt), jnp.zeros((), dt))
        scores = jnp.einsum('bid,bjd->bij', q, k) * D[None]
        return jnp.einsum('bij,bjd->bid', scores, v)

    def _L0_xattn_ref(query, key, value, wq, bq, wk, bk, wv, bv, wo, bo):
        import jax, jax.numpy as jnp
        import numpy as np
        INF = 10000000000.0
        D_MODEL = 256
        N_HEADS = 16
        SCALE = float(np.sqrt(D_MODEL))
        B, S, D = query.shape
        H = N_HEADS
        dh = D // H
        q = query @ wq + bq
        k = key @ wk + bk
        v = value @ wv + bv
        q = q.reshape(B, S, H, dh)
        k = k.reshape(B, S, H, dh)
        v = v.reshape(B, S, H, dh)
        scores = jnp.einsum('bqhd,bkhd->bhqk', q, k)
        causal = jnp.triu(jnp.ones((S, S), scores.dtype), k=1) * INF
        scores = scores - causal
        attn = jax.nn.softmax(scores / SCALE, axis=-1)
        out = jnp.einsum('bhqk,bkhd->bqhd', attn, v).reshape(B, S, D)
        return out @ wo + bo

    def _L0_ffn_ref(inputs, gate_w, w1, w2):
        import jax, jax.numpy as jnp
        import numpy as np
        CAPACITY_FACTOR = 1.25
        orig_shape = inputs.shape
        D = orig_shape[-1]
        tokens = inputs.reshape(-1, D)
        T = tokens.shape[0]
        E = gate_w.shape[0]
        C = int(CAPACITY_FACTOR * T / E)
        logits = tokens @ gate_w.T
        probs = jax.nn.softmax(logits, axis=-1)
        expert_idx = jnp.argmax(probs, axis=-1)
        mask = jax.nn.one_hot(expert_idx, E, dtype=jnp.int32)
        locations = jnp.cumsum(mask, axis=0) - 1
        mask = mask * (locations < C)
        loc_oh = jax.nn.one_hot(locations, C, dtype=probs.dtype)
        sec_mask = mask[:, :, None].astype(probs.dtype) * loc_oh
        combine_weights = probs[:, :, None] * sec_mask
        dispatch = jnp.einsum('tec,td->ecd', sec_mask, tokens)
        h = jax.nn.relu(jnp.einsum('ecd,edh->ech', dispatch, w1))
        expert_out = jnp.einsum('ech,ehd->ecd', h, w2)
        ans = jnp.einsum('tec,ecd->td', combine_weights, expert_out)
        return ans.reshape(orig_shape)
    x = x + _L0_attn_ref(_layernorm(x, axis=-1), L0_attn_weight_q, L0_attn_weight_k, L0_attn_weight_v, L0_attn_theta)
    x = x + _L0_xattn_ref(_layernorm(x, axis=-1), ctx_1024, ctx_1024, L0_xattn_wq, L0_xattn_bq, L0_xattn_wk, L0_xattn_bk, L0_xattn_wv, L0_xattn_bv, L0_xattn_wo, L0_xattn_bo)
    x = x + _L0_ffn_ref(_layernorm(x, axis=-1), L0_ffn_gate_w, L0_ffn_w1, L0_ffn_w2)
    return x

_drawn_inputs = setup_inputs


def setup_inputs(seed=0):
    import zlib

    import numpy as np

    out = dict(_drawn_inputs(seed))
    spreads = {'L0_xattn_bq': (0.0, 0.484),
     'L0_xattn_bk': (0.0, 0.8),
     'L0_xattn_bv': (0.0, 0.1),
     'L0_xattn_bo': (0.0, 0.1)}
    factors = {}
    for name, (base, spread) in spreads.items():
        noise = np.random.default_rng([zlib.crc32(name.encode()), seed]).standard_normal(out[name].shape)
        drawn = base * np.exp(spread * noise) if base else spread * noise
        out[name] = jnp.asarray(drawn.astype(out[name].dtype))
    for name, factor in factors.items():
        out[name] = (out[name] * factor).astype(out[name].dtype)
    return out
```

```python
from contextlib import ExitStack

import concourse.bass as bass
from concourse import mybir

ALU = mybir.AluOpType
ACT = mybir.ActivationFunctionType
AX = mybir.AxisListType.X
F32 = mybir.dt.float32
BF16 = mybir.dt.bfloat16
I32 = mybir.dt.int32
U32 = mybir.dt.uint32

P = 128
B, S, D = 8, 256, 256
KD = D // P
TOK = B * S
NT = TOK // P
PAIRS = B // 2
PT = 2 * S
TPP = PT // P
H, DH = 16, 16
HG = P // DH
G = H // HG
U = 4
NU = H // U
PARTS = 3
COMBOS = ((0, 0), (0, 1), (1, 0), (1, 1), (0, 2), (2, 0))
KS = len(COMBOS) * DH
KM = KS + 2
VW = 32
E, F = 16, 1024
FT = F // P
CAP = int(1.25 * TOK / E)
HALF = CAP // 2
SLOTS = E * CAP
REC = D + 4
FAR = float(1 << 20)
EPS = 1e-5
NEG = -1e30
WR = 4

C_ID, C_DECAY, C_MASK, C_BEFORE, C_IOTA, C_TOK = 0, 128, 384, 512, 640, 656
C_END = C_TOK + NT


def decoder_layer(nc, x, ctx_in, wq1, wk1, wv1, theta, wq, bq, wk, bk, wv, bv, wo, bo,
                  gate_w, w1, w2, consts, out):
    slots = nc.dram_tensor("slots", (SLOTS, REC), F32, kind="Internal").ap()
    x_v = x.rearrange("b s d -> (b s) d").rearrange("(t p) d -> p t d", p=P)
    ctx_v = ctx_in.rearrange("b s d -> (b s) d").rearrange("(t p) d -> p t d", p=P)
    out_rows = out.rearrange("b s d -> (b s) d")

    with ExitStack() as stack:
        def sb(name, shape, dt=F32):
            return stack.enter_context(nc.sbuf_tensor(name, shape, dt))

        def sem(name):
            return stack.enter_context(nc.semaphore(name))

        bank = [stack.enter_context(nc.psum_tensor(f"bank{i}", [P, 512], F32)) for i in range(8)]

        cst = sb("cst", [P, C_END])
        ident = cst[:, C_ID:C_ID + P]
        decay = cst[:, C_DECAY:C_DECAY + 2 * P]
        iota_e = cst[:, C_IOTA:C_IOTA + E]
        ident_b = sb("ident_b", [P, P], BF16)
        mask_b = sb("mask_b", [P, 4 * P], BF16)
        before_b = sb("before_b", [P, P], BF16)
        ones_b = sb("ones_b", [P, P], BF16)
        wq_s = sb("wq_s", [P, KD, D])
        wk_s = sb("wk_s", [P, KD, D])
        wv_s = sb("wv_s", [P, KD, D])
        wo_s = sb("wo_s", [P, KD, D])
        wq_p = sb("wq_p", [P, KD, G, DH, HG])
        wk_p = sb("wk_p", [P, KD, G, DH, HG])
        gw_s = sb("gw_s", [E, D])
        gwT = sb("gwT", [P, KD, E])
        cols = sb("cols", [P, 3, KD])
        turn = sb("turn", [P, KD])
        bv_s = sb("bv_s", [P, D])
        bo_s = sb("bo_s", [P, D])

        def carver(name, words):
            region, at = sb(name, [P, words]), [0]

            def cut(shape, dt=F32, rows=P):
                size = 1
                for n in shape:
                    size *= n
                size = size // 2 if dt == BF16 else size
                view = region[0:rows, at[0]:at[0] + size]
                at[0] += size
                assert at[0] <= words
                if dt != F32:
                    view = view.bitcast(dt)
                names = [f"a{i}" for i in range(len(shape))]
                sizes = {n: m for n, m in zip(names[1:], shape[1:])}
                return view.rearrange(f"p ({' '.join(names)}) -> p {' '.join(names)}", **sizes)

            def again():
                at[0] = 0
            return cut, again

        cut, again = carver("region_q", 2 * H * PT // 2)
        wqk1 = cut([2, KD, D])
        wqk1T = cut([2, KD, D])
        gram = cut([KD, D])
        wv1_s = cut([KD, D])
        xn1 = cut([TPP, D])
        uT = cut([KD, PT])
        v1 = cut([TPP, D])
        pr = cut([2, 3 * P])
        again()
        qst = cut([2, H, PT], BF16, KM)
        again()
        xd = cut([3, 2, REC], F32, HALF)
        xdn = cut([2, D], F32, HALF)
        xdT = cut([KD, CAP])
        hT = cut([FT, CAP])
        yT = cut([KD, CAP])
        yo = cut([2, 2, D], F32, HALF)
        cut, again = carver("region_k", 2 * H * PT // 2)
        kst = cut([2, H, PT], BF16, KM)
        again()
        w_slot2 = (cut([KD, F]), cut([FT, D]))
        w_slot3 = (cut([KD, F]), cut([FT, D]))
        cut, again = carver("region_v", 2 * TPP * H * VW)
        va = cut([2, TPP, H, VW])
        again()
        w_slot1 = (cut([KD, F]), cut([FT, D]))
        w_slot0 = (sb("w1_first", [P, KD, F])[:], sb("w2_first", [P, FT, D])[:])
        w1_s, w2_s = zip(w_slot0, w_slot1, w_slot2, w_slot3)

        xs = sb("xs", [P, NT, D])
        cx = sb("cx", [P, TPP, D])
        stats = sb("stats", [P, TPP, 6])
        mv = sb("mv", [P, 2, NT, 2])
        rstd = sb("rstd", [P, 2, NT])
        vare = sb("vare", [P, TPP])
        mhalf = sb("mhalf", [P, TPP])
        xn2 = sb("xn2", [P, 2, TPP, D])
        xT = sb("xT", [P, KD, PT])
        cT = sb("cT", [P, KD, PT])
        qk = sb("qk", [P, G, PT])
        parts = sb("parts", [P, 2, G, PARTS, PT], BF16)
        mx = sb("mx", [P, 2, 2, H])
        mrow = sb("mrow", [H, 2, S], BF16)
        pT = sb("pT", [P, 6, 512])
        oT = sb("oT", [P, 2, NU, S])
        rden = sb("rden", [P, 2, H])
        o_n = sb("o_n", [P, 2, D])
        oT2 = sb("oT2", [P, 2, KD, P])
        rec = sb("rec", [P, 4, REC])
        st3 = sb("st3", [P, 2, 6])
        var3 = sb("var3", [P, 2, 1])
        x3n = sb("x3n", [P, 2, D])
        x3T = sb("x3T", [P, 2, KD, P])
        top = sb("top", [P, 2, 8])
        topi = sb("topi", [P, 2, 8], U32)
        gsm = sb("gsm", [P, 2, 8])
        gexp = sb("gexp", [P, 2, E])
        hot = sb("hot", [P, 2, E], BF16)
        hotf = sb("hotf", [P, 2, E])
        seen = sb("seen", [P, 4, E], BF16)
        slot_u = sb("slot_u", [P, NT], U32)
        blank = sb("blank", [P, REC])

        cst_in, wa_in, wb_in, sm_in = sem("cst_in"), sem("wa_in"), sem("wb_in"), sem("sm_in")
        x_in = [sem(f"x_in{p}") for p in range(PAIRS)]
        c_in = [sem(f"c_in{p}") for p in range(PAIRS)]
        stack_in = [sem(f"stack_in{i}") for i in range(4)]
        max_in = [sem(f"max_in{i}") for i in range(2)]
        blank_out, row_out = sem("blank_out"), [sem(f"row_out{i}") for i in range(4)]
        scattered = [sem(f"scattered{i}") for i in range(4)]
        w1_in = [sem(f"w1_in{i}") for i in range(WR)]
        w2_in = [sem(f"w2_in{i}") for i in range(WR)]
        xd_in = [sem(f"xd_in{i}") for i in range(3)]
        final_out = [sem(f"final_out{i}") for i in range(2)]
        blank_ok, half_ok, ones_ok, cast_ok, turn_ok = (sem("blank_ok"), sem("half_ok"), sem("ones_ok"),
                                                        sem("cast_ok"), sem("turn_ok"))
        wT_pe, wT_ok, gram_pe, gram_ok = sem("wT_pe"), sem("wT_ok"), sem("gram_pe"), sem("gram_ok")
        dve_c, pool_c, act_c = sem("dve_c"), sem("pool_c"), sem("act_c")
        stat1, rstd1, xn1_ok = sem("stat1"), sem("rstd1"), sem("xn1_ok")
        stat2, rstd2, xn2_ok = sem("stat2"), sem("rstd2"), sem("xn2_ok")
        t1_pe, t1_act, t1_dve = sem("t1_pe"), sem("t1_act"), sem("t1_dve")
        u_pe, u_act, u_dve = sem("u_pe"), sem("u_act"), sem("u_dve")
        v_pe, v_act, v_dve = sem("v_pe"), sem("v_act"), sem("v_dve")
        s1_pe, pr_ok, o1_pe, x1_ok, xb_ok = sem("s1_pe"), sem("pr_ok"), sem("o1_pe"), sem("x1_ok"), sem("xb_ok")
        pj_pe, pj_act, pj_dve, split_ok = sem("pj_pe"), sem("pj_act"), sem("pj_dve"), sem("split_ok")
        s_pe, s_max, m_pe, m_ok = sem("s_pe"), sem("s_max"), sem("m_pe"), sem("m_ok")
        st_pe, exp_ok, sel_ok, pv_pe, ot_ok = sem("st_pe"), sem("exp_ok"), sem("sel_ok"), sem("pv_pe"), sem("ot_ok")
        e1_pe, on_ok, e2_pe, oT2_ok, e3_pe, x3_ok = (sem("e1_pe"), sem("on_ok"), sem("e2_pe"), sem("oT2_ok"),
                                                     sem("e3_pe"), sem("x3_ok"))
        rstd3, x3n_ok, e4_pe, x3T_ok, e5_pe = sem("rstd3"), sem("x3n_ok"), sem("e4_pe"), sem("x3T_ok"), sem("e5_pe")
        seen_ok, kone_in, perm_ok = sem("seen_ok"), sem("kone_in"), sem("perm_ok")
        hot_ok, gexp_ok, e6_pe, slot_ok = sem("hot_ok"), sem("gexp_ok"), sem("e6_pe"), sem("slot_ok")
        xdn_ok, xdT_pe, xdT_ok = sem("xdn_ok"), sem("xdT_pe"), sem("xdT_ok")
        h_pe, h_act, h_dve, y_pe, yT_ok = sem("h_pe"), sem("h_act"), sem("h_dve"), sem("y_pe"), sem("yT_ok")
        z_pe, yo_ok = sem("z_pe"), sem("yo_ok")

        block = stack.enter_context(nc.Block())

        def kt(w):
            return w.rearrange("(k p) n -> p k n", p=P)

        @block.sync
        def _(sp):
            sp.dma_start(cst[:], consts).then_inc(cst_in, 16)
            sp.dma_start(xs[:, 0:TPP, :], x_v[:, 0:TPP, :]).then_inc(x_in[0], 16)
            sp.dma_start(wqk1[:, 0], kt(wq1)).then_inc(wa_in, 16)
            sp.dma_start(wqk1[:, 1], kt(wk1)).then_inc(wa_in, 16)
            sp.dma_start(wv1_s[:], kt(wv1)).then_inc(wa_in, 16)
            with nc.allow_non_contiguous_dma(reason="256 numbers, one a partition"):
                sp.dma_start(cols[:, 0, :], theta.rearrange("(k p) -> p k", p=P)).then_inc(sm_in, 16)
                for i, w in ((1, bq), (2, bk)):
                    for g in range(G):
                        sp.dma_start(cols[:, i, g:g + 1], w[g * P:(g + 1) * P].rearrange("(h d) -> d h", h=HG)
                                     ).then_inc(sm_in, 16)
            for p in range(1, PAIRS):
                sp.dma_start(xs[:, TPP * p:TPP * (p + 1), :], x_v[:, TPP * p:TPP * (p + 1), :]).then_inc(x_in[p], 16)
            for w_s, w in ((wq_s, wq), (wk_s, wk), (wv_s, wv), (wo_s, wo)):
                sp.dma_start(w_s[:], kt(w)).then_inc(wb_in, 16)
            sp.dma_start(bv_s[:], bv.rearrange("(a n) -> a n", a=1).to_broadcast((P, D))).then_inc(wb_in, 16)
            sp.dma_start(bo_s[:], bo.rearrange("(a n) -> a n", a=1).to_broadcast((P, D))).then_inc(wb_in, 16)
            sp.dma_start(gw_s[:], gate_w).then_inc(wb_in, 16)
            sp.dma_start(cx[:], ctx_v[:, 0:TPP, :]).then_inc(c_in[0], 16)
            sp.wait_ge(ones_ok, 1)
            for r in range(2):
                sp.dma_start(kst[KS + r:KS + r + 1].rearrange("r a h t -> r (a h t)"), ones_b[:]).then_inc(kone_in, 16)
            sp.wait_ge(blank_ok, 2)
            sp.dma_start(slots.rearrange("(p j) r -> p j r", p=P),
                         blank[:].rearrange("p (a r) -> p a r", a=1).to_broadcast((P, SLOTS // P, REC))
                         ).then_inc(blank_out, 16)

            def load_w(e):
                s = e % WR
                if e == 1:
                    sp.wait_ge(pv_pe, NU * B)
                elif e in (2, 3):
                    sp.wait_ge(st_pe, 3 * NU * B)
                elif e >= WR:
                    sp.wait_ge(h_pe, 3 * (e - WR + 1))
                sp.dma_start(w1_s[s], w1[e].rearrange("(k p) f -> p k f", p=P)).then_inc(w1_in[s], 16)
                if e >= WR:
                    sp.wait_ge(y_pe, e - WR + 1)
                sp.dma_start(w2_s[s], w2[e].rearrange("(j p) d -> p j d", p=P)).then_inc(w2_in[s], 16)

            load_w(0)

            def project(p, i):
                if i == 4 and p + 1 < PAIRS:
                    sp.wait_ge(pj_pe, 10 * p + 4)
                    sp.dma_start(cx[:], ctx_v[:, TPP * (p + 1):TPP * (p + 2), :]).then_inc(c_in[p + 1], 16)
                if 5 <= i <= 8:
                    which, g = (i - 5) // 2, (i - 5) % 2
                    sp.wait_ge(split_ok, (2 * p + which) * G + g + 1)
                    if i == 5 and p >= 2:
                        sp.wait_ge(st_pe, 3 * NU * 2 * (p - 1))
                    for c, combo in enumerate(COMBOS):
                        dst = (qst, kst)[which][c * DH:(c + 1) * DH, p % 2, g * HG:(g + 1) * HG, :]
                        sp.dma_start(dst, parts[:, which, g, combo[which], :]
                                     ).then_inc(stack_in[p], 16)

            def max_rows(b):
                sp.wait_ge(m_ok, b + 1)
                for r in range(2):
                    sp.dma_start(qst[KS + r:KS + r + 1, (b // 2) % 2, :, (b % 2) * S:(b % 2 + 1) * S], mrow[:, r, :]
                                 ).then_inc(max_in[b % 2], 16)

            def visit(b, k):
                t, v = 2 * b + k % 2, k // 2
                if v == 3:
                    sp.wait_ge(x3_ok, t + 1)
                    sp.dma_start(out_rows[t * P:(t + 1) * P, :], rec[:, t % 4, 0:D]).then_inc(row_out[t % 4], 16)

            for i in range(10):
                project(0, i)
            for s in range(-1, B + 1):
                for u in range(NU):
                    if s >= 1:
                        for j in range(3):
                            visit(s - 1, 3 * u + j)
                    pieces(s, u, project)
                if s + 1 < B:
                    max_rows(s + 1)
                if s == B - 1:
                    load_w(1)
                    load_w(2)
                    load_w(3)
            for i in range(4):
                sp.wait_ge(scattered[i], 16 * (NT // 4))

            def load_x(e):
                if e >= 3:
                    sp.wait_ge(final_out[(e - 3) % 2], 32 * ((e - 3) // 2 + 1))
                sp.dma_start(xd[:, e % 3], slots[e * CAP:(e + 1) * CAP, :].rearrange("(j p) r -> p j r", p=HALF)
                             ).then_inc(xd_in[e % 3], 16)
            for e in range(3):
                load_x(e)
            for e in range(E):
                if e + WR < E:
                    load_w(e + WR)
                if e + 3 < E:
                    load_x(e + 3)

        @block.gpsimd
        def _(pool):
            chain = [0]

            def link(ins):
                chain[0] += 1
                ins.then_inc(pool_c, 1)
                pool.wait_ge(pool_c, chain[0])

            pool.memset(blank[:, 0:D + 3], 0.0).then_inc(blank_ok, 1)
            pool.memset(blank[:, D + 3:REC].bitcast(U32), int(FAR)).then_inc(blank_ok, 1)
            pool.memset(mhalf[:], -0.5).then_inc(half_ok, 1)
            pool.memset(ones_b[:], 1.0).then_inc(ones_ok, 1)
            pool.memset(seen[:, 0, :], 0.0).then_inc(ones_ok, 1)
            pool.wait_ge(half_ok, 1)

            def reciprocal_deviation(dst, var, n):
                link(pool.tensor_scalar(vare[:, 0:n], var, EPS, None, ALU.add))
                return pool.tensor_tensor(dst, vare[:, 0:n], mhalf[:, 0:n], ALU.pow)

            def norm1(p):
                pool.wait_ge(stat1, TPP * (p + 1))
                reciprocal_deviation(rstd[:, 0, TPP * p:TPP * (p + 1)], mv[:, 0, TPP * p:TPP * (p + 1), 1], TPP
                                     ).then_inc(rstd1, 1)
                pool.wait_ge(rstd1, p + 1)

            def norm2(p):
                pool.wait_ge(stat2, TPP * (p + 1))
                reciprocal_deviation(rstd[:, 1, TPP * p:TPP * (p + 1)], mv[:, 1, TPP * p:TPP * (p + 1), 1], TPP
                                     ).then_inc(rstd2, 1)
                pool.wait_ge(rstd2, p + 1)

            def bias_residual(p):
                pool.wait_ge(xn2_ok, p + 1)
                for i in range(TPP):
                    pool.tensor_tensor(xs[:, TPP * p + i, :], xs[:, TPP * p + i, :], bo_s[:], ALU.add
                                       ).then_inc(xb_ok, 1)

            norm1(0)
            va_heads = va.rearrange("p a t h w -> p (a t h) w")
            pool.memset(va_heads[:, :, DH + 1:VW], 0.0).then_inc(ones_ok, 1)
            pool.memset(va_heads[:, :, DH:DH + 1], 1.0).then_inc(ones_ok, 1)
            for p in range(PAIRS):
                if p + 1 < PAIRS:
                    norm1(p + 1)
                if p >= 1:
                    norm2(p - 1)
                if p == 0:
                    pool.wait_ge(wb_in, 16 * 7)
                    for w_to, w_of in ((wq_p, wq_s), (wk_p, wk_s)):
                        for k in range(KD):
                            for g in range(G):
                                pool.tensor_copy(w_to[:, k, g], w_of[:, k, g * P:(g + 1) * P].rearrange(
                                    "p (h d) -> p d h", h=HG)).then_inc(perm_ok, 1)
                if 1 <= p <= 2:
                    bias_residual(p - 1)
            norm2(PAIRS - 1)

            def project(p, i):
                if i == 9 and 2 <= p + 1 < PAIRS:
                    bias_residual(p + 1)

            def select(b, u):
                for j in range(3):
                    n = 3 * (NU * b + u) + j
                    pool.wait_ge(exp_ok, n + 1)
                    if j == 0:
                        view = pT[:, n % 6, :].rearrange("p (h q) -> p h q", h=U)
                        pat = [[0, U], [1, P]]
                    else:
                        view = pT[:, n % 6, :].rearrange("p (h q) -> p h q", h=2)[:, :, 0:P]
                        pat = [[0, 2], [1, P]]
                    pool.affine_select(out=view, in_=view, compare_op=ALU.is_ge, fill=0.0, base=0,
                                       pattern=pat, channel_multiplier=-1).then_inc(sel_ok, 1)

            def norm3(t):
                pool.wait_ge(x3_ok, t + 1)
                q, r = t % 2, t % 4
                link(pool.tensor_scalar(var3[:, q], rec[:, r, D + 1:D + 2], EPS, None, ALU.add))
                pool.tensor_tensor(rec[:, r, D + 1:D + 2], var3[:, q], mhalf[:, 0:1], ALU.pow).then_inc(rstd3, 1)

            def scatter(t):
                pool.wait_ge(slot_ok, t + 1)
                if t == 0:
                    pool.wait_ge(blank_out, 16)
                pool.indirect_dma_start(
                    out=slots, out_offset=bass.IndirectOffsetOnAxis(ap=slot_u[:, t:t + 1], axis=0),
                    in_=rec[:, t % 4, :], in_offset=None, bounds_check=SLOTS - 1, oob_is_err=False
                ).then_inc(scattered[t % 4], 16)

            def visit(b, k):
                t, v = 2 * b + k % 2, k // 2
                if v == 2:
                    norm3(t)
                if v == 5:
                    scatter(t)

            for s in range(-1, B + 1):
                for u in range(NU):
                    if 0 <= s < B:
                        select(s, u)
                    if s >= 1:
                        for j in range(3):
                            visit(s - 1, 3 * u + j)
                    pieces(s, u, project)

            for i in range(4):
                pool.wait_ge(row_out[i], 16 * (NT // 4))
            for e in range(E):
                pool.wait_ge(yo_ok, e + 1)
                for j in range(2):
                    pool.indirect_dma_start(
                        out=out_rows, out_offset=bass.IndirectOffsetOnAxis(
                            ap=xd[:, e % 3, j, D + 3:REC].bitcast(U32), axis=0),
                        in_=yo[:, e % 2, j, :], in_offset=None, bounds_check=TOK - 1, oob_is_err=False
                    ).then_inc(final_out[e % 2], 16)
            pool.wait_ge(final_out[0], 32 * (E // 2))
            pool.wait_ge(final_out[1], 32 * (E // 2))

        @block.scalar
        def _(act):
            def copy(dst, src):
                return act.activation(dst, src, ACT.Copy)

            act.wait_ge(sm_in, 16 * 5)
            act.activation(turn[:], cols[:, 0, :], ACT.Exp, scale=0.0).then_inc(turn_ok, 1)
            for g in range(KD):
                act.wait_ge(gram_pe, g + 1)
                copy(gram[:, g, :], bank[4 + g][:, 0:D]).then_inc(gram_ok, 1)
            for p in range(PAIRS):
                act.wait_ge(t1_pe, 2 * p + 1)
                copy(xT[:, 0, :], bank[0][:]).then_inc(t1_act, 1)
                act.wait_ge(u_pe, 2 * p + 1)
                copy(uT[:, 0, :], bank[2][:]).then_inc(u_act, 1)
                act.wait_ge(v_pe, 2 * p + 1)
                copy(v1[:, 0:2, :].rearrange("p t d -> p (t d)"), bank[4][:]).then_inc(v_act, 1)

            def project(p, i):
                if i >= 8:
                    return
                act.wait_ge(pj_pe, 10 * p + i + 1)
                if i < 4:
                    dst = (xT, cT)[i // 2][:, i % 2, :]
                    copy(dst, bank[7][:]).then_inc(pj_act, 1)
                else:
                    which, g = (i - 4) // 2, i % 2
                    n = (2 * p + which) * G + g
                    if n >= G:
                        act.wait_ge(split_ok, n - G + 1)
                    act.activation(qk[:, g, :], bank[7][:], ACT.Identity,
                                   bias=cols[:, 1 + which, g:g + 1]).then_inc(pj_act, 1)

            def exps(b, u, j):
                n = 3 * (NU * b + u) + j
                act.wait_ge(st_pe, n + 1)
                if n >= 6:
                    act.wait_ge(pv_pe, (n - 6) // 3 + 1)
                act.activation(pT[:, n % 6, :], bank[2 + n % 2][:], ACT.Exp, scale=1.0 / D ** 0.5).then_inc(exp_ok, 1)

            def heads_out(b, u):
                n = NU * b + u
                act.wait_ge(pv_pe, n + 1)
                if b >= 2:
                    act.wait_ge(e1_pe, 2 * (b - 1))
                copy(oT[:, b % 2, u, :], bank[4][:, 0:S]).then_inc(ot_ok, 1)

            def visit(b, k):
                t, v = 2 * b + k % 2, k // 2
                q, bk_ = t % 2, bank[5 + t % 2]
                if v == 1:
                    act.wait_ge(e2_pe, t + 1)
                    copy(oT2[:, q].rearrange("p k t -> p (k t)"), bk_[:, 0:D]).then_inc(oT2_ok, 1)
                if v == 3:
                    act.wait_ge(e4_pe, t + 1)
                    copy(x3T[:, q].rearrange("p k t -> p (k t)"), bk_[:, 0:D]).then_inc(x3T_ok, 1)
                if v == 4:
                    act.wait_ge(hot_ok, t + 1)
                    act.activation(gexp[:, q, :], bk_[:, 0:E], ACT.Exp, bias=gsm[:, q, 1:2],
                                   accum_out=gsm[:, q, 2:3]).then_inc(gexp_ok, 1)

            for i in range(10):
                project(0, i)
            for s in range(-1, B + 1):
                for u in range(NU):
                    for j in range(3):
                        if s >= 1:
                            visit(s - 1, 3 * u + j)
                        if 0 <= s < B:
                            exps(s, u, j)
                    if 0 <= s < B and u >= 1:
                        heads_out(s, u - 1)
                    pieces(s, u, project)
                if 0 <= s < B:
                    heads_out(s, NU - 1)

            def turned(e):
                act.wait_ge(xdT_pe, e + 1)
                copy(xdT.rearrange("p k c -> p (k c)"), bank[0][:, 0:KD * CAP]).then_inc(xdT_ok, 1)

            turned(0)
            for e in range(E):
                for i in (0, 2):
                    act.wait_ge(h_pe, 3 * e + i + 1)
                    n = 3 if i == 0 else 2
                    act.activation(hT[:, 3 * i:3 * i + n, :].rearrange("p f c -> p (f c)"),
                                   bank[1 + i][:, 0:n * CAP], ACT.Relu).then_inc(h_act, 1)
                if e + 1 < E:
                    turned(e + 1)
                act.wait_ge(y_pe, e + 1)
                copy(yT.rearrange("p k c -> p (k c)"), bank[4][:, 0:KD * CAP]).then_inc(yT_ok, 1)

        @block.vector
        def _(dve):
            chain = [0]

            def link(ins):
                chain[0] += 1
                ins.then_inc(dve_c, 1)
                dve.wait_ge(dve_c, chain[0])

            def stats1(p):
                dve.wait_ge(x_in[p], 16)
                for i in range(TPP):
                    dve.bn_stats(stats[:, i, :], xs[:, TPP * p + i, :]).then_inc(dve_c, 1)
                chain[0] += TPP
                dve.wait_ge(dve_c, chain[0])
                for i in range(TPP):
                    dve.bn_aggr(mv[:, 0, TPP * p + i, :], stats[:, i, :]).then_inc(stat1, 1)
                dve.wait_ge(stat1, TPP * (p + 1))

            def apply1(p):
                dve.wait_ge(rstd1, p + 1)
                for i in range(TPP):
                    t = TPP * p + i
                    last = dve.tensor_scalar(xn1[:, i, :], xs[:, t, :], mv[:, 0, t, 0:1], rstd[:, 0, t:t + 1],
                                             ALU.subtract, ALU.mult)
                last.then_inc(xn1_ok, 1)

            def stats2(p):
                for i in range(TPP):
                    dve.bn_stats(stats[:, i, :], xs[:, TPP * p + i, :]).then_inc(dve_c, 1)
                chain[0] += TPP
                dve.wait_ge(dve_c, chain[0])
                for i in range(TPP):
                    dve.bn_aggr(mv[:, 1, TPP * p + i, :], stats[:, i, :]).then_inc(stat2, 1)
                dve.wait_ge(stat2, TPP * (p + 1))

            def apply2(p):
                dve.wait_ge(rstd2, p + 1)
                if p >= 2:
                    dve.wait_ge(pj_pe, 10 * (p - 2) + 2)
                for i in range(TPP):
                    t = TPP * p + i
                    last = dve.tensor_scalar(xn2[:, p % 2, i, :], xs[:, t, :], mv[:, 1, t, 0:1], rstd[:, 1, t:t + 1],
                                             ALU.subtract, ALU.mult)
                last.then_inc(xn2_ok, 1)

            stats1(0)
            dve.wait_ge(cst_in, 16)
            dve.tensor_copy(ident_b[:], ident).then_inc(cast_ok, 1)
            dve.tensor_copy(before_b[:], cst[:, C_BEFORE:C_BEFORE + P]).then_inc(cast_ok, 1)
            for i in range(4):
                dve.tensor_copy(mask_b[:, i * P:(i + 1) * P], cst[:, C_MASK:C_MASK + P]).then_inc(cast_ok, 1)
            apply1(0)
            dve.wait_ge(turn_ok, 1)
            for i in range(4):
                dve.wait_ge(wT_pe, i + 1)
                dve.tensor_scalar(wqk1T[:, i // 2, i % 2, :], bank[i][:, 0:D], turn[:, i % 2:i % 2 + 1], None,
                                  ALU.mult).then_inc(wT_ok, 1)

            def residual1(p):
                for i in range(TPP):
                    dve.wait_ge(o1_pe, TPP * p + 2 * (i // 2) + 2)
                    t = TPP * p + i
                    dve.tensor_tensor(xs[:, t, :], xs[:, t, :], bank[i // 2][:, (i % 2) * D:(i % 2 + 1) * D],
                                      ALU.add).then_inc(x1_ok, 1)
                dve.wait_ge(x1_ok, TPP * (p + 1))

            def decayed(p):
                for i in range(2):
                    dve.wait_ge(s1_pe, 2 * p + i + 1)
                    dve.tensor_tensor(pr[:, i, 0:2 * P], bank[6 + i][:, 0:2 * P], decay, ALU.mult).then_inc(pr_ok, 1)
                    dve.tensor_tensor(pr[:, i, 2 * P:3 * P], bank[6 + i][:, 2 * P:3 * P], decay[:, 0:P],
                                      ALU.mult).then_inc(pr_ok, 1)

            for p in range(PAIRS):
                dve.wait_ge(t1_pe, 2 * p + 2)
                dve.tensor_copy(xT[:, 1, :], bank[1][:]).then_inc(t1_dve, 1)
                dve.wait_ge(u_pe, 2 * p + 2)
                dve.tensor_copy(uT[:, 1, :], bank[3][:]).then_inc(u_dve, 1)
                if p + 1 < PAIRS:
                    stats1(p + 1)
                if p >= 1:
                    residual1(p - 1)
                    stats2(p - 1)
                dve.wait_ge(v_pe, 2 * p + 2)
                dve.tensor_copy(v1[:, 2:4, :].rearrange("p t d -> p (t d)"), bank[5][:]).then_inc(v_dve, 1)
                decayed(p)
                if p + 1 < PAIRS:
                    apply1(p + 1)
                if 1 <= p <= 2:
                    apply2(p - 1)
            residual1(PAIRS - 1)
            stats2(PAIRS - 1)

            dve.wait_ge(wT_pe, 5)
            dve.tensor_copy(gwT[:].rearrange("p k e -> p (k e)"), bank[2][:, 0:KD * E]).then_inc(wT_ok, 1)

            def split(p, which, g):
                dve.wait_ge(pj_act, 8 * p + 4 + 2 * which + g + 1)
                if p >= 1:
                    dve.wait_ge(stack_in[p - 1], 16 * 2 * G * len(COMBOS))
                rest = qk[:, g, :]
                link(dve.tensor_copy(parts[:, which, g, 0, :], rest))
                link(dve.tensor_tensor(rest, rest, parts[:, which, g, 0, :], ALU.subtract))
                link(dve.tensor_copy(parts[:, which, g, 1, :], rest))
                dve.tensor_tensor(parts[:, which, g, 2, :], rest, parts[:, which, g, 1, :], ALU.subtract
                                  ).then_inc(split_ok, 1)

            def project(p, i):
                if 5 <= i <= 8:
                    split(p, (i - 5) // 2, (i - 5) % 2)
                if i >= 8:
                    dve.wait_ge(pj_pe, 10 * p + i + 1)
                    if i == 8:
                        dve.wait_ge(ones_ok, 4)
                        if p >= 2:
                            dve.wait_ge(pv_pe, NU * 2 * (p - 1))
                    for j in range(2):
                        dve.tensor_tensor(
                            va[:, p % 2, 2 * (i - 8) + j, :, 0:DH],
                            bank[7][:, j * D:(j + 1) * D].rearrange("p (h w) -> p h w", h=H),
                            bv_s[:].rearrange("p (h w) -> p h w", h=H), ALU.add).then_inc(pj_dve, 1)
                if i == 9 and 2 <= p + 1 < PAIRS:
                    apply2(p + 1)

            def maxima(b, u, j):
                n = 3 * (NU * b + u) + j
                dve.wait_ge(s_pe, n + 1)
                if u == 0 and j == 0 and b >= 2:
                    dve.wait_ge(m_pe, b - 1)
                if j == 0:
                    dve.tensor_reduce(mx[:, b % 2, 0, U * u:U * u + U],
                                      bank[n % 2][:].rearrange("p (h k) -> p h k", h=U), AX, ALU.max).then_inc(s_max, 1)
                else:
                    h = U * u + 2 * (j - 1)
                    dve.tensor_reduce(mx[:, b % 2, 1, h:h + 2],
                                      bank[n % 2][:].rearrange("p (h k) -> p h k", h=2), AX, ALU.max).then_inc(s_max, 1)

            def maxima_rows(b):
                dve.wait_ge(m_pe, b + 1)
                if b >= 1:
                    dve.wait_ge(max_in[(b - 1) % 2], 32 * ((b - 1) // 2 + 1))
                link(dve.tensor_scalar(mrow[:, 0, :], bank[7][0:H, 0:S], -1.0, None, ALU.mult))
                dve.scalar_tensor_tensor(out=mrow[:, 1, :], in0=bank[7][0:H, 0:S], scalar=-1.0, in1=mrow[:, 0, :],
                                         op0=ALU.mult, op1=ALU.subtract).then_inc(m_ok, 1)

            def visit(b, k):
                t, v = 2 * b + k % 2, k // 2
                q, bk_, r = t % 2, bank[5 + t % 2], t % 4
                if v == 0:
                    dve.wait_ge(e1_pe, t + 1)
                    heads = bk_[:].rearrange("p (h w) -> p h w", w=VW)
                    link(dve.reciprocal(rden[:, q, :].rearrange("p (h a) -> p h a", a=1), heads[:, :, DH:DH + 1]))
                    dve.tensor_tensor(o_n[:, q, :].rearrange("p (h w) -> p h w", w=DH), heads[:, :, 0:DH],
                                      rden[:, q, :].rearrange("p (h a) -> p h a", a=1).to_broadcast((P, H, DH)),
                                      ALU.mult).then_inc(on_ok, 1)
                if v == 2:
                    dve.wait_ge(e3_pe, t + 1)
                    if t >= 4:
                        dve.wait_ge(row_out[r], 16 * (t // 4))
                        dve.wait_ge(scattered[r], 16 * (t // 4))
                    dve.wait_ge(xb_ok, t + 1)
                    link(dve.tensor_tensor(rec[:, r, 0:D], bk_[:, 0:D], xs[:, t, :], ALU.add))
                    link(dve.bn_stats(st3[:, q, :], rec[:, r, 0:D]))
                    dve.bn_aggr(rec[:, r, D:D + 2], st3[:, q, :]).then_inc(x3_ok, 1)
                if v == 3:
                    dve.wait_ge(rstd3, t + 1)
                    dve.tensor_scalar(x3n[:, q, :], rec[:, r, 0:D], rec[:, r, D:D + 1], rec[:, r, D + 1:D + 2],
                                      ALU.subtract, ALU.mult).then_inc(x3n_ok, 1)
                    dve.tensor_copy(rec[:, r, D + 3:REC].bitcast(U32), cst[:, C_TOK + t:C_TOK + t + 1])
                if v == 4:
                    dve.wait_ge(e5_pe, t + 1)
                    link(dve.max(top[:, q, :], bk_[:, 0:E]))
                    link(dve.max_index(topi[:, q, :], top[:, q, :], bk_[:, 0:E]))
                    link(dve.tensor_copy(gsm[:, q, 0:1], topi[:, q, 0:1]))
                    link(dve.tensor_scalar(gsm[:, q, 1:2], top[:, q, 0:1], -1.0, None, ALU.mult))
                    link(dve.tensor_scalar(hotf[:, q, :], iota_e, gsm[:, q, 0:1], None, ALU.is_equal))
                    dve.tensor_copy(hot[:, q, :], hotf[:, q, :]).then_inc(hot_ok, 1)
                    dve.wait_ge(hot_ok, t + 1)
                    if t + 1 < NT:
                        if t >= 3:
                            dve.wait_ge(e6_pe, t - 2)
                        if t == 0:
                            dve.wait_ge(ones_ok, 2)
                        dve.tensor_tensor(seen[:, (t + 1) % 4, :], seen[:, t % 4, :], hot[:, q, :], ALU.add
                                          ).then_inc(seen_ok, 1)
                        dve.wait_ge(seen_ok, t + 1)
                if v == 5:
                    dve.wait_ge(e6_pe, t + 1)
                    dve.wait_ge(gexp_ok, t + 1)
                    dve.reciprocal(rec[:, r, D + 2:D + 3], gsm[:, q, 2:3])
                    link(dve.tensor_tensor(hotf[:, q, :], bk_[:, 32:32 + E], hotf[:, q, :], ALU.mult))
                    link(dve.tensor_reduce(gsm[:, q, 3:4], hotf[:, q, :], AX, ALU.add))
                    dve.tensor_scalar(gsm[:, q, 4:5], gsm[:, q, 3:4], float(CAP), FAR, ALU.is_ge, ALU.mult)
                    link(dve.scalar_tensor_tensor(out=gsm[:, q, 5:6], in0=gsm[:, q, 0:1], scalar=float(CAP),
                                                  in1=gsm[:, q, 3:4], op0=ALU.mult, op1=ALU.add))
                    dve.tensor_tensor(slot_u[:, t:t + 1], gsm[:, q, 4:5], gsm[:, q, 5:6], ALU.add).then_inc(slot_ok, 1)

            for i in range(10):
                project(0, i)
            for s in range(-1, B + 1):
                for u in range(NU):
                    for j in range(3):
                        if s >= 1:
                            visit(s - 1, 3 * u + j)
                        if s + 1 < B:
                            maxima(s + 1, u, j)
                    pieces(s, u, project)
                if s + 1 < B:
                    maxima_rows(s + 1)

            def normalise(e):
                dve.wait_ge(xd_in[e % 3], 16 * (e // 3 + 1))
                if e >= 1:
                    dve.wait_ge(xdT_pe, e)
                for j in range(2):
                    last = dve.tensor_scalar(xdn[:, j, :], xd[:, e % 3, j, 0:D], xd[:, e % 3, j, D:D + 1],
                                             xd[:, e % 3, j, D + 1:D + 2], ALU.subtract, ALU.mult)
                last.then_inc(xdn_ok, 1)

            def finish(e):
                dve.wait_ge(z_pe, e + 1)
                if e >= 2:
                    dve.wait_ge(final_out[e % 2], 32 * (e // 2))
                for j in range(2):
                    last = dve.scalar_tensor_tensor(
                        out=yo[:, e % 2, j, :], in0=bank[5][0:HALF, j * D:(j + 1) * D],
                        scalar=xd[:, e % 3, j, D + 2:D + 3], in1=xd[:, e % 3, j, 0:D], op0=ALU.mult, op1=ALU.add)
                last.then_inc(yo_ok, 1)

            normalise(0)
            for e in range(E):
                if e + 1 < E:
                    normalise(e + 1)
                dve.wait_ge(h_pe, 3 * e + 2)
                dve.tensor_scalar(hT[:, 3:6, :].rearrange("p f c -> p (f c)"), bank[2][:, 0:3 * CAP], 0.0, None,
                                  ALU.max).then_inc(h_dve, 1)
                if e >= 1:
                    finish(e - 1)
            finish(E - 1)

        @block.tensor
        def _(pe):
            pe.wait_ge(cst_in, 16)
            pe.wait_ge(wa_in, 16 * 3)
            for i in range(4):
                w, kc = i // 2, i % 2
                for r in range(KD):
                    last = pe.transpose(bank[i][:, r * P:(r + 1) * P], wqk1[:, w, r, kc * P:(kc + 1) * P], ident)
                last.then_inc(wT_pe, 1)
            pe.wait_ge(wT_ok, 4)
            for m in range(KD):
                for k in range(KD):
                    last = pe.matmul(bank[4 + m][:, 0:D], wqk1T[:, 0, k, m * P:(m + 1) * P], wqk1T[:, 1, k, :],
                                     start=(k == 0), stop=(k == KD - 1))
                last.then_inc(gram_pe, 1)

            def turn_rows(p):
                pe.wait_ge(xn1_ok, p + 1)
                if p >= 2:
                    pe.wait_ge(x1_ok, TPP * (p - 1))
                for k in range(KD):
                    for i in range(TPP):
                        last = pe.transpose(bank[k][:, i * P:(i + 1) * P], xn1[:, i, k * P:(k + 1) * P], ident)
                    last.then_inc(t1_pe, 1)

            def fold(p):
                pe.wait_ge(t1_act, p + 1)
                pe.wait_ge(t1_dve, p + 1)
                if p == 0:
                    pe.wait_ge(gram_ok, KD)
                for m in range(KD):
                    for k in range(KD):
                        last = pe.matmul(bank[2 + m][:], gram[:, k, m * P:(m + 1) * P], xT[:, k, :],
                                         start=(k == 0), stop=(k == KD - 1))
                    last.then_inc(u_pe, 1)

            def values1(p):
                for i in range(TPP):
                    for k in range(KD):
                        last = pe.matmul(bank[4 + i // 2][:, (i % 2) * D:(i % 2 + 1) * D],
                                         xT[:, k, i * P:(i + 1) * P], wv1_s[:, k, :],
                                         start=(k == 0), stop=(k == KD - 1), skip_group_check=True)
                    if i % 2:
                        last.then_inc(v_pe, 1)

            def scores1(p):
                pe.wait_ge(u_act, p + 1)
                pe.wait_ge(u_dve, p + 1)
                for i in range(2):
                    o = i * S
                    for k in range(KD):
                        pe.matmul(bank[6 + i][:, 0:S], xT[:, k, o:o + P], uT[:, k, o:o + S],
                                  start=(k == 0), stop=(k == KD - 1))
                    for k in range(KD):
                        last = pe.matmul(bank[6 + i][:, S:S + P], xT[:, k, o + P:o + S], uT[:, k, o + P:o + S],
                                         start=(k == 0), stop=(k == KD - 1))
                    last.then_inc(s1_pe, 1)

            def retain(p):
                pe.wait_ge(pr_ok, 4 * (p + 1))
                pe.wait_ge(v_act, p + 1)
                pe.wait_ge(v_dve, p + 1)
                for i in range(TPP):
                    b, q = i // 2, i % 2
                    dst = bank[i // 2][:, q * D:(q + 1) * D]
                    last = pe.matmul(dst, pr[:, b, q * P:(q + 1) * P], v1[:, 2 * b, :], start=True, stop=(q == 0))
                    if q == 1:
                        last = pe.matmul(dst, pr[:, b, 2 * P:3 * P], v1[:, 2 * b + 1, :], start=False, stop=True)
                    last.then_inc(o1_pe, 1)

            for p in range(PAIRS):
                turn_rows(p)
                fold(p)
                if p >= 1:
                    retain(p - 1)
                values1(p)
                scores1(p)
            retain(PAIRS - 1)
            pe.wait_ge(wb_in, 16 * 7)
            for k in range(KD):
                last = pe.transpose(bank[2][:, k * E:(k + 1) * E], gw_s[:, k * P:(k + 1) * P], ident[0:E, 0:E])
            last.then_inc(wT_pe, 1)
            pe.wait_ge(cast_ok, 6)
            pe.wait_ge(ones_ok, 4)
            pe.wait_ge(wT_ok, 5)
            pe.wait_ge(pr_ok, 4 * PAIRS)
            pe.wait_ge(x1_ok, NT)
            pe.wait_ge(kone_in, 32)
            pe.wait_ge(perm_ok, 2 * KD * G)

            def project(p, i):
                if i == 9:
                    pe.wait_ge(pj_dve, 4 * p + 2)
                elif 1 <= i <= 8:
                    pe.wait_ge(pj_act, 8 * p + i)
                elif p >= 1:
                    pe.wait_ge(pj_dve, 4 * p)
                if i == 0 and p >= 2:
                    pe.wait_ge(m_ok, 2 * p - 2)
                if i == 5 and p >= 1:
                    pe.wait_ge(m_ok, 2 * p - 1)
                if i < 4:
                    k = i % 2
                    if i == 0:
                        pe.wait_ge(xn2_ok, p + 1)
                    if i == 2:
                        pe.wait_ge(c_in[p], 16)
                    for t in range(TPP):
                        src = (xn2[:, p % 2, t, k * P:(k + 1) * P] if i < 2 else cx[:, t, k * P:(k + 1) * P])
                        last = pe.transpose(bank[7][:, t * P:(t + 1) * P], src, ident)
                elif i < 8:
                    which, g = (i - 4) // 2, i % 2
                    for k in range(KD):
                        last = pe.matmul(bank[7][:], (wq_p, wk_p)[which][:, k, g].rearrange("p d h -> p (d h)"),
                                         (xT, cT)[which][:, k, :], start=(k == 0), stop=(k == KD - 1))
                else:
                    for j in range(2):
                        t = 2 * (i - 8) + j
                        for k in range(KD):
                            last = pe.matmul(bank[7][:, j * D:(j + 1) * D], cT[:, k, t * P:(t + 1) * P],
                                             wv_s[:, k, :], start=(k == 0), stop=(k == KD - 1), skip_group_check=True)
                last.then_inc(pj_pe, 1)

            def scores(b, u, j):
                n = 3 * (NU * b + u) + j
                p, o, dst = b // 2, (b % 2) * S, bank[n % 2]
                if n >= 2:
                    pe.wait_ge(s_max, n - 1)
                if n % (6 * NU) == 0:
                    pe.wait_ge(stack_in[p], 16 * 2 * G * len(COMBOS))
                if j == 0:
                    pe.matmul(dst[:], ident_b[:], mask_b[:], start=True, stop=False, skip_group_check=True)
                    for i in range(U):
                        h = U * u + i
                        last = pe.matmul(dst[:, i * P:(i + 1) * P], qst[0:KS, p % 2, h, o:o + P],
                                         kst[0:KS, p % 2, h, o:o + P], start=False, stop=(i == U - 1),
                                         skip_group_check=True)
                else:
                    pe.matmul(dst[:].rearrange("p (h k) -> p h k", h=2)[:, :, P:S], ident_b[:],
                              mask_b[:, 0:S].rearrange("p (h k) -> p h k", h=2), start=True, stop=False,
                              skip_group_check=True)
                    for i in range(2):
                        h = U * u + 2 * (j - 1) + i
                        last = pe.matmul(dst[:, i * S:(i + 1) * S], qst[0:KS, p % 2, h, o + P:o + S],
                                         kst[0:KS, p % 2, h, o:o + S], start=False, stop=(i == 1),
                                         skip_group_check=True)
                last.then_inc(s_pe, 1)

            def maxima_turned(b):
                pe.wait_ge(s_max, 3 * NU * (b + 1))
                p, later = (b + 2) // 2, (b + 2) % 2
                if p >= PAIRS:
                    p, later = PAIRS - 1, 1
                pe.wait_ge(pj_act, 8 * p + (8 if later else 5))
                pe.wait_ge(pj_dve, 4 * p + 4 * later)
                if b >= 1:
                    pe.wait_ge(m_ok, b)
                for q in range(2):
                    last = pe.transpose(bank[7][0:H, q * P:(q + 1) * P], mx[:, b % 2, q, :], ident)
                last.then_inc(m_pe, 1)

            def shifted(b, u, j):
                n = 3 * (NU * b + u) + j
                p, o, dst = b // 2, (b % 2) * S, bank[2 + n % 2]
                if n >= 2:
                    pe.wait_ge(exp_ok, n - 1)
                if u == 0 and j == 0:
                    pe.wait_ge(max_in[b % 2], 32 * (b // 2 + 1))
                for i in range(U if j == 0 else 2):
                    if j == 0:
                        h = U * u + i
                        last = pe.matmul(dst[:, i * P:(i + 1) * P], kst[:, p % 2, h, o + P:o + S],
                                         qst[:, p % 2, h, o + P:o + S], start=True, stop=True)
                    else:
                        h = U * u + 2 * (j - 1) + i
                        last = pe.matmul(dst[:, i * S:(i + 1) * S], kst[:, p % 2, h, o:o + P],
                                         qst[:, p % 2, h, o:o + S], start=True, stop=True)
                last.then_inc(st_pe, 1)

            def weigh(b, u):
                n = NU * b + u
                pe.wait_ge(sel_ok, 3 * (n + 1))
                if n >= 1:
                    pe.wait_ge(ot_ok, n)
                if u == 0 and b % 2 == 0:
                    pe.wait_ge(pj_dve, 4 * (b // 2 + 1))
                for kt_ in range(2):
                    for i in range(U):
                        lhs = va[:, (b // 2) % 2, 2 * (b % 2) + kt_, U * u + i, :]
                        if kt_ == 0:
                            rhs = pT[:, (3 * n + 1 + i // 2) % 6, (i % 2) * S:(i % 2 + 1) * S]
                            dst = bank[4][VW * i:VW * (i + 1), 0:S]
                        else:
                            rhs = pT[:, (3 * n) % 6, i * P:(i + 1) * P]
                            dst = bank[4][VW * i:VW * (i + 1), P:S]
                        last = pe.matmul(dst, lhs, rhs, start=(kt_ == 0), stop=(kt_ == 1), skip_group_check=True)
                last.then_inc(pv_pe, 1)

            def visit(b, k):
                t, v = 2 * b + k % 2, k // 2
                q, dst = t % 2, bank[5 + t % 2]
                if v == 0:
                    pe.wait_ge(ot_ok, NU * (b + 1))
                    if t >= 2:
                        pe.wait_ge(slot_ok, t - 1)
                    for u in range(NU):
                        last = pe.transpose(dst[:, u * P:(u + 1) * P], oT[:, b % 2, u, q * P:(q + 1) * P], ident)
                    last.then_inc(e1_pe, 1)
                if v == 1:
                    pe.wait_ge(on_ok, t + 1)
                    for k_ in range(KD):
                        last = pe.transpose(dst[:, k_ * P:(k_ + 1) * P], o_n[:, q, k_ * P:(k_ + 1) * P], ident)
                    last.then_inc(e2_pe, 1)
                if v == 2:
                    pe.wait_ge(oT2_ok, t + 1)
                    for k_ in range(KD):
                        last = pe.matmul(dst[:, 0:D], oT2[:, q, k_, :], wo_s[:, k_, :], start=(k_ == 0),
                                         stop=(k_ == KD - 1))
                    last.then_inc(e3_pe, 1)
                if v == 3:
                    pe.wait_ge(x3n_ok, t + 1)
                    for k_ in range(KD):
                        last = pe.transpose(dst[:, k_ * P:(k_ + 1) * P], x3n[:, q, k_ * P:(k_ + 1) * P], ident)
                    last.then_inc(e4_pe, 1)
                if v == 4:
                    pe.wait_ge(x3T_ok, t + 1)
                    for k_ in range(KD):
                        last = pe.matmul(dst[:, 0:E], x3T[:, q, k_, :], gwT[:, k_, :], start=(k_ == 0),
                                         stop=(k_ == KD - 1))
                    last.then_inc(e5_pe, 1)
                if v == 5:
                    pe.wait_ge(hot_ok, t + 1)
                    pe.wait_ge(gexp_ok, t + 1)
                    if t >= 1:
                        pe.wait_ge(seen_ok, t)
                    pe.matmul(dst[:, 32:32 + E], before_b[:], hot[:, q, :], start=True, stop=False)
                    pe.matmul(dst[:, 32:32 + E], ones_b[:], seen[:, t % 4, :], start=False, stop=True
                              ).then_inc(e6_pe, 1)

            for i in range(10):
                project(0, i)
            for s in range(-1, B + 1):
                for u in range(NU):
                    for j in range(3):
                        if s >= 1:
                            visit(s - 1, 3 * u + j)
                        if s + 1 < B:
                            scores(s + 1, u, j)
                        if 0 <= s < B:
                            shifted(s, u, j)
                    if 0 <= s < B and u >= 1:
                        weigh(s, u - 1)
                    pieces(s, u, project)
                if 0 <= s < B:
                    weigh(s, NU - 1)
                if s + 1 < B:
                    maxima_turned(s + 1)

            def turn_slots(e):
                pe.wait_ge(xdn_ok, e + 1)
                for k in range(KD):
                    for j in range(2):
                        last = pe.transpose(bank[0][:, k * CAP + j * HALF:k * CAP + (j + 1) * HALF],
                                            xdn[:, j, k * P:(k + 1) * P], ident[0:HALF, 0:HALF])
                last.then_inc(xdT_pe, 1)

            def hidden(e):
                pe.wait_ge(xdT_ok, e + 1)
                pe.wait_ge(w1_in[e % WR], 16 * (e // WR + 1))
                for f in range(FT):
                    for k in range(KD):
                        last = pe.matmul(bank[1 + f // 3][:, (f % 3) * CAP:(f % 3 + 1) * CAP],
                                         w1_s[e % WR][:, k, f * P:(f + 1) * P], xdT[:, k, :],
                                         start=(k == 0), stop=(k == KD - 1), skip_group_check=True)
                    if f % 3 == 2 or f == FT - 1:
                        last.then_inc(h_pe, 1)

            def back(e):
                pe.wait_ge(yT_ok, e + 1)
                if e >= 1:
                    pe.wait_ge(yo_ok, e)
                for j in range(2):
                    for k in range(KD):
                        last = pe.transpose(bank[5][0:HALF, j * D + k * P:j * D + (k + 1) * P],
                                            yT[:, k, j * HALF:(j + 1) * HALF], ident)
                last.then_inc(z_pe, 1)

            def outward(e):
                pe.wait_ge(w2_in[e % WR], 16 * (e // WR + 1))
                for k in range(KD):
                    for f in range(FT):
                        if k == 0 and f in (0, 6):
                            pe.wait_ge(h_act, 2 * e + 1 + (f == 6))
                        if k == 0 and f == 3:
                            pe.wait_ge(h_dve, e + 1)
                        last = pe.matmul(bank[4][:, k * CAP:(k + 1) * CAP], w2_s[e % WR][:, f, k * P:(k + 1) * P],
                                         hT[:, f, :], start=(f == 0), stop=(f == FT - 1), skip_group_check=True)
                last.then_inc(y_pe, 1)

            turn_slots(0)
            for e in range(E):
                hidden(e)
                if e >= 1:
                    back(e - 1)
                if e + 1 < E:
                    turn_slots(e + 1)
                outward(e)
            back(E - 1)


def pieces(s, u, project):
    p = (s + 3) // 2
    at = ((s + 3) % 2) * NU + u
    if not 1 <= p < PAIRS or s < -1:
        return
    for i in ((0,), (1,), (2, 3), (4,), (5,), (6,), (7,), (8, 9))[at]:
        project(p, i)


_INS = ['x', 'ctx_1024', 'L0_attn_weight_q', 'L0_attn_weight_k', 'L0_attn_weight_v', 'L0_attn_theta',
        'L0_xattn_wq', 'L0_xattn_bq', 'L0_xattn_wk', 'L0_xattn_bk', 'L0_xattn_wv', 'L0_xattn_bv',
        'L0_xattn_wo', 'L0_xattn_bo', 'L0_ffn_gate_w', 'L0_ffn_w1', 'L0_ffn_w2']


def constants():
    import numpy as np
    r, c = np.arange(P)[:, None], np.arange(P)[None, :]
    q = np.arange(2 * P)[None, :]
    decay = np.where(q >= r, np.float32(0.96875) ** np.maximum(q - r, 0).astype(np.float32), 0)
    return np.concatenate([
        np.eye(P), decay, np.where(c > r, NEG, 0), (r < c), np.broadcast_to(np.arange(E)[None, :], (P, E)),
        r + P * np.arange(NT)[None, :]], axis=1).astype(np.float32)


def kernel(**inputs):
    import numpy as _np
    import concourse.bacc as _bacc
    from concourse import mybir as _mybir
    from concourse.bass_utils import run_bass_kernel_spmd as _run

    nc = _bacc.Bacc("TRN2", target_bir_lowering=False, num_devices=1)
    arrays, args = {}, []
    for name, a in [(n, inputs[n]) for n in _INS] + [("constants", constants())]:
        a = _np.ascontiguousarray(a)
        arrays[f"in_{name}_dram"] = a
        args.append(nc.dram_tensor(f"in_{name}_dram", a.shape, _mybir.dt.from_np(a.dtype), kind="ExternalInput").ap())
    out = nc.dram_tensor("out_0_dram", (B, S, D), _mybir.dt.float32, kind="ExternalOutput").ap()
    decoder_layer(nc, *args, out)
    r = _run(nc, [arrays], core_ids=[0])
    return r.results[0]["out_0_dram"]
```

```python
from contextlib import ExitStack

import concourse.bass as bass
from concourse import mybir

ALU = mybir.AluOpType
ACT = mybir.ActivationFunctionType
AX = mybir.AxisListType.X
F32 = mybir.dt.float32
BF16 = mybir.dt.bfloat16
U32 = mybir.dt.uint32

P = 128
B, S, D = 8, 256, 256
KD = D // P
TOK = B * S
NT = TOK // P
PAIRS = B // 2
PT = 2 * S
TPP = PT // P
H, DH = 16, 16
HG = P // DH
G = H // HG
STACKED = 16 * 2 * G * 6
U = 4
NU = H // U
PARTS = 3
COMBOS = ((0, 0), (0, 1), (1, 0), (1, 1), (0, 2), (2, 0))
KS = len(COMBOS) * DH
KM = KS + 2
VW = 32
E, F = 16, 1024
FT = F // P
CAP = int(1.25 * TOK / E)
HALF = CAP // 2
SLOTS = E * CAP
REC = D + 4
FAR = float(1 << 20)
EPS = 1e-5
NEG = -1e30
WR = 4

C_ID, C_DECAY, C_MASK, C_BEFORE, C_IOTA, C_TOK = 0, 128, 384, 512, 640, 656
C_END = C_TOK + NT


def decoder_layer(nc, x, ctx_in, wq1, wk1, wv1, theta, wq, bq, wk, bk, wv, bv, wo, bo,
                  gate_w, w1, w2, consts, out):
    slots = nc.dram_tensor("slots", (SLOTS, REC), F32, kind="Internal").ap()
    x_v = x.rearrange("b s d -> (b s) d").rearrange("(t p) d -> p t d", p=P)
    ctx_v = ctx_in.rearrange("b s d -> (b s) d").rearrange("(t p) d -> p t d", p=P)
    out_rows = out.rearrange("b s d -> (b s) d")

    with ExitStack() as stack:
        def sb(name, shape, dt=F32):
            return stack.enter_context(nc.sbuf_tensor(name, shape, dt))

        def sem(name):
            return stack.enter_context(nc.semaphore(name))

        bank = [stack.enter_context(nc.psum_tensor(f"bank{i}", [P, 512], F32))[:] for i in range(5)]
        pair = stack.enter_context(nc.psum_tensor("pair", [P, 2, 512], F32))
        bank += [pair[:, 0, :], pair[:, 1, :], stack.enter_context(nc.psum_tensor("bank7", [P, 512], F32))[:]]

        cst = sb("cst", [P, C_END])
        ident = cst[:, C_ID:C_ID + P]
        decay = cst[:, C_DECAY:C_DECAY + 2 * P]
        iota_e = cst[:, C_IOTA:C_IOTA + E]
        ident_b = sb("ident_b", [P, P], BF16)
        mask_b = sb("mask_b", [P, 4 * P], BF16)
        before_b = sb("before_b", [P, P], BF16)
        ones_b = sb("ones_b", [P, P], BF16)
        wq_s = sb("wq_s", [P, KD, D])
        wk_s = sb("wk_s", [P, KD, D])
        wv_s = sb("wv_s", [P, KD, D])
        wo_s = sb("wo_s", [P, KD, D])
        wq_p = sb("wq_p", [P, KD, G, DH, HG])
        wk_p = sb("wk_p", [P, KD, G, DH, HG])
        gw_s = sb("gw_s", [E, D])
        gwT = sb("gwT", [P, KD, E])
        cols = sb("cols", [P, 3, KD])
        turn = sb("turn", [P, KD])
        bv_s = sb("bv_s", [P, D])
        bo_s = sb("bo_s", [P, D])

        def carver(name, words):
            region, at = sb(name, [P, words]), [0]

            def cut(shape, dt=F32, rows=P):
                size = 1
                for n in shape:
                    size *= n
                size = size // 2 if dt == BF16 else size
                view = region[0:rows, at[0]:at[0] + size]
                at[0] += size
                assert at[0] <= words
                if dt != F32:
                    view = view.bitcast(dt)
                names = [f"a{i}" for i in range(len(shape))]
                sizes = {n: m for n, m in zip(names[1:], shape[1:])}
                return view.rearrange(f"p ({' '.join(names)}) -> p {' '.join(names)}", **sizes)

            def again(word):
                at[0] = word
            return cut, again

        cut, again = carver("region_q", 2 * H * PT // 2)
        qst = cut([2, H, PT], BF16, KM)
        again(H * PT // 2)
        xn1 = cut([TPP, D])
        uT = cut([KD, PT])
        v1 = cut([TPP, D])
        pr = cut([2, 3 * P])
        again(0)
        xd = cut([3, 2, REC], F32, HALF)
        xdn = cut([2, D], F32, HALF)
        xdT = cut([KD, CAP])
        hT = cut([FT, CAP])
        yT = cut([KD, CAP])
        yo = cut([2, 2, D], F32, HALF)
        cut, again = carver("region_k", 2 * H * PT // 2)
        kst = cut([2, H, PT], BF16, KM)
        again(0)
        w_slot2 = (cut([KD, F]), cut([FT, D]))
        w_slot3 = (cut([KD, F]), cut([FT, D]))
        cut, again = carver("region_v", 2 * TPP * H * VW)
        va = cut([2, TPP, H, VW])
        again(0)
        w_slot1 = (cut([KD, F]), cut([FT, D]))
        cut, again = carver("region_w", KD * F + FT * D)
        wqk1 = cut([2, KD, D])
        wqk1T = cut([2, KD, D])
        gram = cut([KD, D])
        wv1_s = cut([KD, D])
        again(0)
        w_slot0 = (cut([KD, F]), cut([FT, D]))
        w1_s, w2_s = zip(w_slot0, w_slot1, w_slot2, w_slot3)

        xs = sb("xs", [P, NT, D])
        cx = sb("cx", [P, TPP, D])
        stats = sb("stats", [P, TPP, 6])
        mv = sb("mv", [P, 2, NT, 2])
        rstd = sb("rstd", [P, 2, NT])
        vare = sb("vare", [P, TPP])
        mhalf = sb("mhalf", [P, TPP])
        xn2 = sb("xn2", [P, 2, TPP, D])
        xT = sb("xT", [P, KD, PT])
        cT = sb("cT", [P, KD, PT])
        qk = sb("qk", [P, G, PT])
        parts = sb("parts", [P, 2, G, PARTS, PT], BF16)
        mx = sb("mx", [P, 2, 2, H])
        mrow = sb("mrow", [H, 2, S], BF16)
        pT = sb("pT", [P, 6, 512])
        oT = sb("oT", [P, 2, NU, S])
        rden = sb("rden", [P, 2, H])
        o_n = sb("o_n", [P, 2, D])
        oT2 = sb("oT2", [P, 2, KD, P])
        rec = sb("rec", [P, 2, 2, REC])
        st3 = sb("st3", [P, 2, 6])
        var3 = sb("var3", [P, 2, 1])
        x3n = sb("x3n", [P, 2, D])
        x3T = sb("x3T", [P, 2, KD, P])
        top = sb("top", [P, 2, 8])
        topi = sb("topi", [P, 2, 8], U32)
        gsm = sb("gsm", [P, 6, 2])
        gexp = sb("gexp", [P, 2, E])
        hot = sb("hot", [P, 2, E], BF16)
        ahead = sb("ahead", [P, 2, E])
        seen = sb("seen", [P, 2, E], BF16)
        slot_u = sb("slot_u", [P, NT], U32)
        blank = sb("blank", [P, REC])

        cst_in, wa_in, wb_in, sm_in = sem("cst_in"), sem("wa_in"), sem("wb_in"), sem("sm_in")
        x_in = [sem(f"x_in{p}") for p in range(PAIRS)]
        c_in = [sem(f"c_in{p}") for p in range(PAIRS)]
        stack_in = [sem(f"stack_in{i}") for i in range(4)]
        max_in = [sem(f"max_in{i}") for i in range(2)]
        blank_out, row_out = sem("blank_out"), [sem(f"row_out{i}") for i in range(2)]
        scattered = [sem(f"scattered{i}") for i in range(2)]
        w1_in = [sem(f"w1_in{i}") for i in range(WR)]
        w2_in = [sem(f"w2_in{i}") for i in range(WR)]
        xd_in = [sem(f"xd_in{i}") for i in range(3)]
        final_out = [sem(f"final_out{i}") for i in range(2)]
        id_in, wv_in = sem("id_in"), sem("wv_in")
        blank_ok, half_ok, ones_ok, cast_ok, turn_ok = (sem("blank_ok"), sem("half_ok"), sem("ones_ok"),
                                                        sem("cast_ok"), sem("turn_ok"))
        wT_pe, wT_ok, gram_pe, gram_ok = sem("wT_pe"), sem("wT_ok"), sem("gram_pe"), sem("gram_ok")
        dve_c, pool_c, act_c = sem("dve_c"), sem("pool_c"), sem("act_c")
        stat1, rstd1, xn1_ok = sem("stat1"), sem("rstd1"), sem("xn1_ok")
        stat2, rstd2, xn2_ok = sem("stat2"), sem("rstd2"), sem("xn2_ok")
        t1_pe, t1_act, t1_dve = sem("t1_pe"), sem("t1_act"), sem("t1_dve")
        u_pe, u_act, u_dve = sem("u_pe"), sem("u_act"), sem("u_dve")
        v_pe, v_act, v_dve = sem("v_pe"), sem("v_act"), sem("v_dve")
        s1_pe, pr_ok, o1_pe, x1_ok, xb_ok = sem("s1_pe"), sem("pr_ok"), sem("o1_pe"), sem("x1_ok"), sem("xb_ok")
        pj_pe, pj_act, pj_dve, split_ok = sem("pj_pe"), sem("pj_act"), sem("pj_dve"), sem("split_ok")
        rest_ok = sem("rest_ok")
        s_pe, s_max, m_pe, m_ok = sem("s_pe"), sem("s_max"), sem("m_pe"), sem("m_ok")
        st_pe, exp_ok, sel_ok, pv_pe, ot_ok = sem("st_pe"), sem("exp_ok"), sem("sel_ok"), sem("pv_pe"), sem("ot_ok")
        e1_pe, on_ok, e2_pe, oT2_ok, e3_pe, x3_ok = (sem("e1_pe"), sem("on_ok"), sem("e2_pe"), sem("oT2_ok"),
                                                     sem("e3_pe"), sem("x3_ok"))
        rstd3, x3n_ok, e4_pe, x3T_ok, e5_pe = sem("rstd3"), sem("x3n_ok"), sem("e4_pe"), sem("x3T_ok"), sem("e5_pe")
        seen_ok, kone_in, perm_ok = sem("seen_ok"), sem("kone_in"), sem("perm_ok")
        hot_ok, gexp_ok, e6_pe, slot_ok = sem("hot_ok"), sem("gexp_ok"), sem("e6_pe"), sem("slot_ok")
        xdn_ok, xdT_pe, xdT_ok = sem("xdn_ok"), sem("xdT_pe"), sem("xdT_ok")
        h_pe, h_act, h_dve, y_pe, yT_ok = sem("h_pe"), sem("h_act"), sem("h_dve"), sem("y_pe"), sem("yT_ok")
        z_pe, yo_ok = sem("z_pe"), sem("yo_ok")

        block = stack.enter_context(nc.Block())

        def piece_bank(p, i):
            return bank[7] if p else bank[2 + i % 2]

        def kt(w):
            return w.rearrange("(k p) n -> p k n", p=P)

        @block.sync
        def _(sp):
            sp.dma_start(xs[:, 0:TPP, :], x_v[:, 0:TPP, :]).then_inc(x_in[0], 16)
            sp.dma_start(wqk1[:, 1], kt(wk1)).then_inc(wa_in, 16)
            sp.dma_start(cst[:, C_DECAY:C_END], consts[:, C_DECAY:C_END]).then_inc(cst_in, 16)
            sp.dma_start(wv1_s[:], kt(wv1)).then_inc(wv_in, 16)
            sp.dma_start(gw_s[:], gate_w).then_inc(wv_in, 16)
            with nc.allow_non_contiguous_dma(reason="256 numbers, one a partition"):
                sp.dma_start(cols[:, 0, :], theta.rearrange("(k p) -> p k", p=P)).then_inc(sm_in, 16)
                for i, w in ((1, bq), (2, bk)):
                    for g in range(G):
                        sp.dma_start(cols[:, i, g:g + 1], w[g * P:(g + 1) * P].rearrange("(h d) -> d h", h=HG)
                                     ).then_inc(sm_in, 16)
            for p in range(1, PAIRS):
                sp.dma_start(xs[:, TPP * p:TPP * (p + 1), :], x_v[:, TPP * p:TPP * (p + 1), :]).then_inc(x_in[p], 16)
            for w_s, w in ((wq_s, wq), (wk_s, wk), (wv_s, wv), (wo_s, wo)):
                sp.dma_start(w_s[:], kt(w)).then_inc(wb_in, 16)
            sp.dma_start(bv_s[:], bv.rearrange("(a n) -> a n", a=1).to_broadcast((P, D))).then_inc(wb_in, 16)
            sp.dma_start(bo_s[:], bo.rearrange("(a n) -> a n", a=1).to_broadcast((P, D))).then_inc(wb_in, 16)
            sp.dma_start(cx[:], ctx_v[:, 0:TPP, :]).then_inc(c_in[0], 16)
            sp.wait_ge(ones_ok, 1)
            for r in range(2):
                sp.dma_start(kst[KS + r:KS + r + 1].rearrange("r a h t -> r (a h t)"), ones_b[:]).then_inc(kone_in, 16)
            sp.wait_ge(blank_ok, 2)
            sp.dma_start(slots.rearrange("(p j) r -> p j r", p=P),
                         blank[:].rearrange("p (a r) -> p a r", a=1).to_broadcast((P, SLOTS // P, REC))
                         ).then_inc(blank_out, 16)

            def load_w(e):
                s = e % WR
                if e == 1:
                    sp.wait_ge(pv_pe, NU * B)
                elif e in (2, 3):
                    sp.wait_ge(st_pe, 3 * NU * B)
                elif e >= WR:
                    sp.wait_ge(h_pe, 3 * (e - WR + 1))
                sp.dma_start(w1_s[s], w1[e].rearrange("(k p) f -> p k f", p=P)).then_inc(w1_in[s], 16)
                if e >= WR:
                    sp.wait_ge(y_pe, e - WR + 1)
                sp.dma_start(w2_s[s], w2[e].rearrange("(j p) d -> p j d", p=P)).then_inc(w2_in[s], 16)

            def project(p, i):
                if i == 4 and p + 1 < PAIRS:
                    sp.wait_ge(pj_pe, 10 * p + 4)
                    sp.dma_start(cx[:], ctx_v[:, TPP * (p + 1):TPP * (p + 2), :]).then_inc(c_in[p + 1], 16)
                if 5 <= i <= 8:
                    which, g = (i - 5) // 2, (i - 5) % 2
                    sp.wait_ge(split_ok, (2 * p + which) * G + g + 1)
                    if i == 5 and p >= 2:
                        sp.wait_ge(st_pe, 3 * NU * 2 * (p - 1))
                    for c, combo in enumerate(COMBOS):
                        dst = (qst, kst)[which][c * DH:(c + 1) * DH, p % 2, g * HG:(g + 1) * HG, :]
                        sp.dma_start(dst, parts[:, which, g, combo[which], :]
                                     ).then_inc(stack_in[p], 16)

            def max_rows(b):
                sp.wait_ge(m_ok, b + 1)
                for r in range(2):
                    sp.dma_start(qst[KS + r:KS + r + 1, (b // 2) % 2, :, (b % 2) * S:(b % 2 + 1) * S], mrow[:, r, :]
                                 ).then_inc(max_in[b % 2], 16)

            def visit(b, v):
                if v == 3:
                    sp.wait_ge(x3_ok, b + 1)
                    sp.dma_start(out_rows[b * S:(b + 1) * S, :].rearrange("(q p) d -> p q d", p=P), rec[:, b % 2, :, 0:D]
                                 ).then_inc(row_out[b % 2], 16)

            for i in range(10):
                project(0, i)
            sp.wait_ge(o1_pe, NT)
            load_w(0)
            for T in STEPS:
                for b, v in visits_at(T):
                    visit(b, v)
                if piece_at(T):
                    project(*piece_at(T))
                if scored_at(T) and scored_at(T)[1] == LAST:
                    max_rows(scored_at(T)[0])
            load_w(1)
            for i in range(2):
                sp.wait_ge(scattered[i], 16 * 2 * (B // 2))

            def load_x(e):
                if e >= 3:
                    sp.wait_ge(final_out[(e - 3) % 2], 32 * ((e - 3) // 2 + 1))
                sp.dma_start(xd[:, e % 3], slots[e * CAP:(e + 1) * CAP, :].rearrange("(j p) r -> p j r", p=HALF)
                             ).then_inc(xd_in[e % 3], 16)
            for e in range(3):
                load_x(e)
            load_w(2)
            load_w(3)
            for e in range(E):
                if e + WR < E:
                    load_w(e + WR)
                if e + 3 < E:
                    load_x(e + 3)

        @block.gpsimd
        def _(pool):
            chain = [0]

            def link(ins):
                chain[0] += 1
                ins.then_inc(pool_c, 1)
                pool.wait_ge(pool_c, chain[0])

            pool.memset(blank[:, 0:D + 3], 0.0).then_inc(blank_ok, 1)
            pool.memset(blank[:, D + 3:REC].bitcast(U32), int(FAR)).then_inc(blank_ok, 1)
            pool.memset(mhalf[:], -0.5).then_inc(half_ok, 1)
            pool.memset(ones_b[:], 1.0).then_inc(ones_ok, 1)
            pool.memset(seen[:, 0, :], 0.0).then_inc(ones_ok, 1)
            pool.wait_ge(half_ok, 1)

            def reciprocal_deviation(dst, var, n):
                link(pool.tensor_scalar(vare[:, 0:n], var, EPS, None, ALU.add))
                return pool.tensor_tensor(dst, vare[:, 0:n], mhalf[:, 0:n], ALU.pow)

            def norm1(p):
                pool.wait_ge(stat1, TPP * (p + 1))
                reciprocal_deviation(rstd[:, 0, TPP * p:TPP * (p + 1)], mv[:, 0, TPP * p:TPP * (p + 1), 1], TPP
                                     ).then_inc(rstd1, 1)
                pool.wait_ge(rstd1, p + 1)

            def norm2(p):
                pool.wait_ge(stat2, TPP * (p + 1))
                reciprocal_deviation(rstd[:, 1, TPP * p:TPP * (p + 1)], mv[:, 1, TPP * p:TPP * (p + 1), 1], TPP
                                     ).then_inc(rstd2, 1)
                pool.wait_ge(rstd2, p + 1)

            def bias_residual(p):
                pool.wait_ge(xn2_ok, p + 1)
                for i in range(TPP):
                    pool.tensor_tensor(xs[:, TPP * p + i, :], xs[:, TPP * p + i, :], bo_s[:], ALU.add
                                       ).then_inc(xb_ok, 1)

            norm1(0)
            va_heads = va.rearrange("p a t h w -> p (a t h) w")
            pool.memset(va_heads[:, :, DH + 1:VW], 0.0).then_inc(ones_ok, 1)
            pool.memset(va_heads[:, :, DH:DH + 1], 1.0).then_inc(ones_ok, 1)

            def retention(p):
                if p + 1 < PAIRS:
                    norm1(p + 1)
                if p >= 1:
                    norm2(p - 1)
                if p == 0:
                    pool.wait_ge(wb_in, 16 * 6)
                    for w_to, w_of in ((wq_p, wq_s), (wk_p, wk_s)):
                        for k in range(KD):
                            for g in range(G):
                                pool.tensor_copy(w_to[:, k, g], w_of[:, k, g * P:(g + 1) * P].rearrange(
                                    "p (h d) -> p d h", h=HG)).then_inc(perm_ok, 1)
                if 1 <= p <= 2:
                    bias_residual(p - 1)

            def project(p, i):
                if 5 <= i <= 8:
                    which, g = (i - 5) // 2, (i - 5) % 2
                    n = (2 * p + which) * G + g
                    pool.wait_ge(pj_act, 8 * p + 4 + 2 * which + g + 1)
                    pool.tensor_tensor(qk[:, g, :], qk[:, g, :], parts[:, which, g, 0, :], ALU.subtract
                                       ).then_inc(rest_ok, 1)
                if i == 9 and 2 <= p + 1 < PAIRS:
                    bias_residual(p + 1)

            def select(b, u, j):
                n = 3 * (NU * b + u) + j
                pool.wait_ge(exp_ok, n + 1)
                heads = U if j == 0 else 2
                view = pT[:, n % 6, :].rearrange("p (h q) -> p h q", h=heads)[:, :, 0:P]
                pool.affine_select(out=view, in_=view, compare_op=ALU.is_ge, fill=0.0, base=0,
                                   pattern=[[0, heads], [1, P]], channel_multiplier=-1).then_inc(sel_ok, 1)

            def norm3(b):
                pool.wait_ge(x3_ok, b + 1)
                link(pool.tensor_scalar(var3[:], rec[:, b % 2, :, D + 1:D + 2], EPS, None, ALU.add))
                pool.tensor_tensor(rec[:, b % 2, :, D + 1:D + 2], var3[:],
                                   mhalf[:, 0:2].rearrange("p (q a) -> p q a", a=1), ALU.pow).then_inc(rstd3, 1)

            def scatter(b):
                pool.wait_ge(slot_ok, b + 1)
                if b == 0:
                    pool.wait_ge(blank_out, 16)
                for q in range(2):
                    t = 2 * b + q
                    pool.indirect_dma_start(
                        out=slots, out_offset=bass.IndirectOffsetOnAxis(ap=slot_u[:, t:t + 1], axis=0),
                        in_=rec[:, b % 2, q, :], in_offset=None, bounds_check=SLOTS - 1, oob_is_err=False
                    ).then_inc(scattered[b % 2], 16)

            for p in range(PAIRS):
                retention(p)
                if p == FIRST_PROJECTED:
                    for i in range(10):
                        project(0, i)
            norm2(PAIRS - 1)
            for T in STEPS:
                if weighed_at(T):
                    b, k = weighed_at(T)
                    select(b, k // 3, k % 3)
                for b, v in visits_at(T):
                    if v == NORM:
                        norm3(b)
                    if v == 5:
                        scatter(b)
                if piece_at(T):
                    project(*piece_at(T))

            for i in range(2):
                pool.wait_ge(row_out[i], 16 * (B // 2))
            for e in range(E):
                pool.wait_ge(yo_ok, e + 1)
                for j in range(2):
                    pool.indirect_dma_start(
                        out=out_rows, out_offset=bass.IndirectOffsetOnAxis(
                            ap=xd[:, e % 3, j, D + 3:REC].bitcast(U32), axis=0),
                        in_=yo[:, e % 2, j, :], in_offset=None, bounds_check=TOK - 1, oob_is_err=False
                    ).then_inc(final_out[e % 2], 16)
            pool.wait_ge(final_out[0], 32 * (E // 2))
            pool.wait_ge(final_out[1], 32 * (E // 2))

        @block.scalar
        def _(act):
            chain = [0]

            def link(ins):
                chain[0] += 1
                ins.then_inc(act_c, 1)
                act.wait_ge(act_c, chain[0])

            def copy(dst, src):
                return act.activation(dst, src, ACT.Copy)

            act.dma_start(cst[:, 0:P], consts[:, 0:P]).then_inc(id_in, 16)
            act.dma_start(wqk1[:, 0], kt(wq1)).then_inc(wa_in, 16)
            act.wait_ge(sm_in, 16 * 5)
            act.activation(turn[:], cols[:, 0, :], ACT.Exp, scale=0.0).then_inc(turn_ok, 1)
            for g in range(KD):
                act.wait_ge(gram_pe, g + 1)
                copy(gram[:, g, :], bank[4 + g][:, 0:D]).then_inc(gram_ok, 1)

            def retention(p):
                act.wait_ge(t1_pe, 2 * p + 1)
                copy(xT[:, 0, :], bank[0]).then_inc(t1_act, 1)
                act.wait_ge(u_pe, 2 * p + 1)
                copy(uT[:, 0, :], bank[2]).then_inc(u_act, 1)
                act.wait_ge(v_pe, 2 * p + 1)
                copy(v1[:, 0:2, :].rearrange("p t d -> p (t d)"), bank[4]).then_inc(v_act, 1)

            def project(p, i):
                if i >= 8:
                    return
                act.wait_ge(pj_pe, 10 * p + i + 1)
                if i < 4:
                    dst = (xT, cT)[i // 2][:, i % 2, :]
                    copy(dst, piece_bank(p, i)).then_inc(pj_act, 1)
                else:
                    which, g = (i - 4) // 2, i % 2
                    n = (2 * p + which) * G + g
                    if n >= G:
                        act.wait_ge(split_ok, n - G + 1)
                    if p >= 1:
                        act.wait_ge(stack_in[p - 1], STACKED)
                    link(act.activation(qk[:, g, :], piece_bank(p, i), ACT.Identity,
                                        bias=cols[:, 1 + which, g:g + 1]))
                    act.activation(parts[:, which, g, 0, :], piece_bank(p, i), ACT.Identity,
                                   bias=cols[:, 1 + which, g:g + 1]).then_inc(pj_act, 1)

            def exps(b, u, j):
                n = 3 * (NU * b + u) + j
                act.wait_ge(st_pe, n + 1)
                if n >= 6:
                    act.wait_ge(pv_pe, (n - 6) // 3 + 1)
                act.activation(pT[:, n % 6, :], bank[2 + n % 2], ACT.Exp, scale=1.0 / D ** 0.5).then_inc(exp_ok, 1)

            def heads_out(b, u):
                n = NU * b + u
                act.wait_ge(pv_pe, n + 1)
                if b >= 2:
                    act.wait_ge(e1_pe, b - 1)
                copy(oT[:, b % 2, u, :], bank[4][:, 0:S]).then_inc(ot_ok, 1)

            def visit(b, v):
                if v == 1:
                    act.wait_ge(e2_pe, b + 1)
                    copy(oT2[:].rearrange("p q k t -> p q (k t)"), pair[:, :, 0:D]).then_inc(oT2_ok, 1)
                if v == 3:
                    act.wait_ge(e4_pe, b + 1)
                    copy(x3T[:].rearrange("p q k t -> p q (k t)"), pair[:, :, 0:D]).then_inc(x3T_ok, 1)
                if v == 4:
                    act.wait_ge(hot_ok, b + 1)
                    for q in range(2):
                        act.activation(gexp[:, q, :], pair[:, q, 0:E], ACT.Exp, bias=gsm[:, 1, q:q + 1],
                                       accum_out=gsm[:, 2, q:q + 1]).then_inc(gexp_ok, 1)

            for p in range(PAIRS):
                retention(p)
                if p == FIRST_PROJECTED:
                    for i in range(10):
                        project(0, i)
            for T in STEPS:
                if weighed_at(T):
                    b, k = weighed_at(T)
                    exps(b, k // 3, k % 3)
                if sums_at(T - 1) is not None:
                    heads_out(*divmod(sums_at(T - 1), NU))
                for b, v in visits_at(T):
                    visit(b, v)
                if piece_at(T):
                    project(*piece_at(T))

            def turned(e):
                act.wait_ge(xdT_pe, e + 1)
                copy(xdT.rearrange("p k c -> p (k c)"), bank[0][:, 0:KD * CAP]).then_inc(xdT_ok, 1)

            turned(0)
            for e in range(E):
                for i in (0, 2):
                    act.wait_ge(h_pe, 3 * e + i + 1)
                    n = 3 if i == 0 else 2
                    act.activation(hT[:, 3 * i:3 * i + n, :].rearrange("p f c -> p (f c)"),
                                   bank[1 + i][:, 0:n * CAP], ACT.Relu).then_inc(h_act, 1)
                if e + 1 < E:
                    turned(e + 1)
                act.wait_ge(y_pe, e + 1)
                copy(yT.rearrange("p k c -> p (k c)"), bank[4][:, 0:KD * CAP]).then_inc(yT_ok, 1)

        @block.vector
        def _(dve):
            chain = [0]

            def link(ins):
                chain[0] += 1
                ins.then_inc(dve_c, 1)
                dve.wait_ge(dve_c, chain[0])

            def stats1(p):
                dve.wait_ge(x_in[p], 16)
                for i in range(TPP):
                    dve.bn_stats(stats[:, i, :], xs[:, TPP * p + i, :]).then_inc(dve_c, 1)
                chain[0] += TPP
                dve.wait_ge(dve_c, chain[0])
                for i in range(TPP):
                    dve.bn_aggr(mv[:, 0, TPP * p + i, :], stats[:, i, :]).then_inc(stat1, 1)
                dve.wait_ge(stat1, TPP * (p + 1))

            def apply1(p):
                dve.wait_ge(rstd1, p + 1)
                for i in range(TPP):
                    t = TPP * p + i
                    last = dve.tensor_scalar(xn1[:, i, :], xs[:, t, :], mv[:, 0, t, 0:1], rstd[:, 0, t:t + 1],
                                             ALU.subtract, ALU.mult)
                last.then_inc(xn1_ok, 1)

            def stats2(p):
                for i in range(TPP):
                    dve.bn_stats(stats[:, i, :], xs[:, TPP * p + i, :]).then_inc(dve_c, 1)
                chain[0] += TPP
                dve.wait_ge(dve_c, chain[0])
                for i in range(TPP):
                    dve.bn_aggr(mv[:, 1, TPP * p + i, :], stats[:, i, :]).then_inc(stat2, 1)
                dve.wait_ge(stat2, TPP * (p + 1))

            def apply2(p):
                dve.wait_ge(rstd2, p + 1)
                if p >= 2:
                    dve.wait_ge(pj_pe, 10 * (p - 2) + 2)
                for i in range(TPP):
                    t = TPP * p + i
                    last = dve.tensor_scalar(xn2[:, p % 2, i, :], xs[:, t, :], mv[:, 1, t, 0:1], rstd[:, 1, t:t + 1],
                                             ALU.subtract, ALU.mult)
                last.then_inc(xn2_ok, 1)

            stats1(0)
            dve.wait_ge(cst_in, 16)
            dve.wait_ge(id_in, 16)
            dve.tensor_copy(ident_b[:], ident).then_inc(cast_ok, 1)
            dve.tensor_copy(before_b[:], cst[:, C_BEFORE:C_BEFORE + P]).then_inc(cast_ok, 1)
            for i in range(4):
                dve.tensor_copy(mask_b[:, i * P:(i + 1) * P], cst[:, C_MASK:C_MASK + P]).then_inc(cast_ok, 1)
            apply1(0)
            dve.wait_ge(turn_ok, 1)
            for i in range(4):
                dve.wait_ge(wT_pe, i + 1)
                dve.tensor_scalar(wqk1T[:, i // 2, i % 2, :], bank[i][:, 0:D], turn[:, i % 2:i % 2 + 1], None,
                                  ALU.mult).then_inc(wT_ok, 1)
            dve.wait_ge(wT_pe, 5)
            dve.tensor_copy(gwT[:].rearrange("p k e -> p (k e)"), bank[6][:, 0:KD * E]).then_inc(wT_ok, 1)

            def residual1(p):
                for i in range(TPP):
                    dve.wait_ge(o1_pe, TPP * p + 2 * (i // 2) + 2)
                    t = TPP * p + i
                    dve.tensor_tensor(xs[:, t, :], xs[:, t, :], bank[i // 2][:, (i % 2) * D:(i % 2 + 1) * D],
                                      ALU.add).then_inc(x1_ok, 1)
                dve.wait_ge(x1_ok, TPP * (p + 1))

            def decayed(p):
                for i in range(2):
                    dve.wait_ge(s1_pe, 2 * p + i + 1)
                    dve.tensor_tensor(pr[:, i, 0:2 * P], bank[6 + i][:, 0:2 * P], decay, ALU.mult).then_inc(pr_ok, 1)
                    dve.tensor_tensor(pr[:, i, 2 * P:3 * P], bank[6 + i][:, 2 * P:3 * P], decay[:, 0:P],
                                      ALU.mult).then_inc(pr_ok, 1)

            def retention(p):
                dve.wait_ge(t1_pe, 2 * p + 2)
                dve.tensor_copy(xT[:, 1, :], bank[1]).then_inc(t1_dve, 1)
                if p + 1 < PAIRS:
                    stats1(p + 1)
                dve.wait_ge(u_pe, 2 * p + 2)
                dve.tensor_copy(uT[:, 1, :], bank[3]).then_inc(u_dve, 1)
                if p + 1 < PAIRS:
                    apply1(p + 1)
                if p >= 1:
                    residual1(p - 1)
                    stats2(p - 1)
                dve.wait_ge(v_pe, 2 * p + 2)
                dve.tensor_copy(v1[:, 2:4, :].rearrange("p t d -> p (t d)"), bank[5]).then_inc(v_dve, 1)
                decayed(p)
                if 1 <= p <= 2:
                    apply2(p - 1)

            def split(p, which, g):
                dve.wait_ge(rest_ok, (2 * p + which) * G + g + 1)
                link(dve.tensor_copy(parts[:, which, g, 1, :], qk[:, g, :]))
                dve.tensor_tensor(parts[:, which, g, 2, :], qk[:, g, :], parts[:, which, g, 1, :], ALU.subtract
                                  ).then_inc(split_ok, 1)

            def project(p, i):
                if 5 <= i <= 8:
                    split(p, (i - 5) // 2, (i - 5) % 2)
                if i >= 8:
                    dve.wait_ge(pj_pe, 10 * p + i + 1)
                    if i == 8:
                        dve.wait_ge(ones_ok, 4)
                        if p >= 2:
                            dve.wait_ge(pv_pe, NU * 2 * (p - 1))
                    for j in range(2):
                        dve.tensor_tensor(
                            va[:, p % 2, 2 * (i - 8) + j, :, 0:DH],
                            piece_bank(p, i)[:, j * D:(j + 1) * D].rearrange("p (h w) -> p h w", h=H),
                            bv_s[:].rearrange("p (h w) -> p h w", h=H), ALU.add).then_inc(pj_dve, 1)
                if i == 9 and 2 <= p + 1 < PAIRS:
                    apply2(p + 1)

            def maxima(b, u, j):
                n = 3 * (NU * b + u) + j
                dve.wait_ge(s_pe, n + 1)
                if u == 0 and j == 0 and b >= 2:
                    dve.wait_ge(m_pe, b - 1)
                if j == 0:
                    dve.tensor_reduce(mx[:, b % 2, 0, U * u:U * u + U],
                                      bank[n % 2].rearrange("p (h k) -> p h k", h=U), AX, ALU.max).then_inc(s_max, 1)
                else:
                    h = U * u + 2 * (j - 1)
                    dve.tensor_reduce(mx[:, b % 2, 1, h:h + 2],
                                      bank[n % 2].rearrange("p (h k) -> p h k", h=2), AX, ALU.max).then_inc(s_max, 1)

            def maxima_rows(b):
                dve.wait_ge(m_pe, b + 1)
                if b >= 1:
                    dve.wait_ge(max_in[(b - 1) % 2], 32 * ((b - 1) // 2 + 1))
                link(dve.tensor_scalar(mrow[:, 0, :], bank[7][0:H, 0:S], -1.0, None, ALU.mult))
                dve.scalar_tensor_tensor(out=mrow[:, 1, :], in0=bank[7][0:H, 0:S], scalar=-1.0, in1=mrow[:, 0, :],
                                         op0=ALU.mult, op1=ALU.subtract).then_inc(m_ok, 1)

            def visit(b, v):
                r = b % 2
                if v == 0:
                    dve.wait_ge(e1_pe, b + 1)
                    heads = pair[:].rearrange("p q (h w) -> p (q h) w", w=VW)
                    link(dve.reciprocal(rden[:].rearrange("p q (h a) -> p (q h) a", a=1), heads[:, :, DH:DH + 1]))
                    dve.tensor_tensor(o_n[:].rearrange("p q (h w) -> p (q h) w", w=DH), heads[:, :, 0:DH],
                                      rden[:].rearrange("p q (h a) -> p (q h) a", a=1).to_broadcast((P, 2 * H, DH)),
                                      ALU.mult).then_inc(on_ok, 1)
                if v == 2:
                    dve.wait_ge(e3_pe, b + 1)
                    if b >= 2:
                        dve.wait_ge(row_out[r], 16 * (b // 2))
                        dve.wait_ge(scattered[r], 32 * (b // 2))
                    dve.wait_ge(xb_ok, 2 * b + 2)
                    link(dve.tensor_tensor(rec[:, r, :, 0:D], pair[:, :, 0:D], xs[:, 2 * b:2 * b + 2, :], ALU.add))
                    for q in range(2):
                        dve.bn_stats(st3[:, q, :], rec[:, r, q, 0:D]).then_inc(dve_c, 1)
                    chain[0] += 2
                    dve.wait_ge(dve_c, chain[0])
                    dve.bn_aggr(rec[:, r, 0, D:D + 2], st3[:, 0, :])
                    dve.bn_aggr(rec[:, r, 1, D:D + 2], st3[:, 1, :]).then_inc(x3_ok, 1)
                if v == APPLY:
                    dve.wait_ge(rstd3, b + 1)
                    for q in range(2):
                        last = dve.tensor_scalar(x3n[:, q, :], rec[:, r, q, 0:D], rec[:, r, q, D:D + 1],
                                                 rec[:, r, q, D + 1:D + 2], ALU.subtract, ALU.mult)
                    last.then_inc(x3n_ok, 1)
                    dve.tensor_copy(rec[:, r, :, D + 3:REC].bitcast(U32),
                                    cst[:, C_TOK + 2 * b:C_TOK + 2 * b + 2].rearrange("p (q a) -> p q a", a=1))
                if v == 4:
                    dve.wait_ge(e5_pe, b + 1)
                    for q in range(2):
                        dve.max(top[:, q, :], pair[:, q, 0:E]).then_inc(dve_c, 1)
                    chain[0] += 2
                    dve.wait_ge(dve_c, chain[0])
                    for q in range(2):
                        dve.max_index(topi[:, q, :], top[:, q, :], pair[:, q, 0:E]).then_inc(dve_c, 1)
                    chain[0] += 2
                    dve.tensor_scalar(gsm[:, 1, :], top[:, :, 0], -1.0, None, ALU.mult)
                    dve.wait_ge(dve_c, chain[0])
                    link(dve.tensor_copy(gsm[:, 0, :], topi[:, :, 0]))
                    dve.tensor_tensor(hot[:], iota_e.rearrange("p (a e) -> p a e", a=1).to_broadcast((P, 2, E)),
                                      gsm[:, 0, :].rearrange("p (q a) -> p q a", a=1).to_broadcast((P, 2, E)),
                                      ALU.is_equal).then_inc(hot_ok, 1)
                if v == 5:
                    dve.wait_ge(e6_pe, b + 1)
                    dve.wait_ge(gexp_ok, 2 * b + 2)
                    dve.wait_ge(hot_ok, b + 1)
                    dve.reciprocal(rec[:, r, :, D + 2:D + 3], gsm[:, 2, :].rearrange("p (q a) -> p q a", a=1))
                    link(dve.tensor_tensor(ahead[:], pair[:, :, 32:32 + E], hot[:], ALU.mult))
                    link(dve.tensor_reduce(gsm[:, 3, :], ahead[:], AX, ALU.add))
                    dve.tensor_scalar(gsm[:, 4, :], gsm[:, 3, :], float(CAP), FAR, ALU.is_ge, ALU.mult)
                    link(dve.scalar_tensor_tensor(out=gsm[:, 5, :], in0=gsm[:, 0, :], scalar=float(CAP),
                                                  in1=gsm[:, 3, :], op0=ALU.mult, op1=ALU.add))
                    dve.tensor_tensor(slot_u[:, 2 * b:2 * b + 2], gsm[:, 4, :], gsm[:, 5, :], ALU.add
                                      ).then_inc(slot_ok, 1)
                    if b + 1 < B:
                        if b == 0:
                            dve.wait_ge(ones_ok, 2)
                        link(dve.tensor_tensor(ahead[:, 0, :], hot[:, 0, :], hot[:, 1, :], ALU.add))
                        dve.tensor_tensor(seen[:, (b + 1) % 2, :], seen[:, b % 2, :], ahead[:, 0, :], ALU.add
                                          ).then_inc(seen_ok, 1)

            for p in range(PAIRS):
                retention(p)
                if p == FIRST_PROJECTED:
                    for i in range(10):
                        project(0, i)
            residual1(PAIRS - 1)
            stats2(PAIRS - 1)
            for T in STEPS:
                if scored_at(T):
                    b, k = scored_at(T)
                    maxima(b, k // 3, k % 3)
                    if k == LAST:
                        maxima_rows(b)
                for b, v in visits_at(T):
                    visit(b, v)
                if piece_at(T):
                    project(*piece_at(T))

            def normalise(e):
                dve.wait_ge(xd_in[e % 3], 16 * (e // 3 + 1))
                if e >= 1:
                    dve.wait_ge(xdT_pe, e)
                for j in range(2):
                    last = dve.tensor_scalar(xdn[:, j, :], xd[:, e % 3, j, 0:D], xd[:, e % 3, j, D:D + 1],
                                             xd[:, e % 3, j, D + 1:D + 2], ALU.subtract, ALU.mult)
                last.then_inc(xdn_ok, 1)

            def finish(e):
                dve.wait_ge(z_pe, e + 1)
                if e >= 2:
                    dve.wait_ge(final_out[e % 2], 32 * (e // 2))
                for j in range(2):
                    last = dve.scalar_tensor_tensor(
                        out=yo[:, e % 2, j, :], in0=bank[5][0:HALF, j * D:(j + 1) * D],
                        scalar=xd[:, e % 3, j, D + 2:D + 3], in1=xd[:, e % 3, j, 0:D], op0=ALU.mult, op1=ALU.add)
                last.then_inc(yo_ok, 1)

            normalise(0)
            for e in range(E):
                if e + 1 < E:
                    normalise(e + 1)
                dve.wait_ge(h_pe, 3 * e + 2)
                dve.tensor_scalar(hT[:, 3:6, :].rearrange("p f c -> p (f c)"), bank[2][:, 0:3 * CAP], 0.0, None,
                                  ALU.max).then_inc(h_dve, 1)
                if e >= 1:
                    finish(e - 1)
            finish(E - 1)

        @block.tensor
        def _(pe):
            pe.wait_ge(id_in, 16)
            pe.wait_ge(wa_in, 16 * 2)
            for i in range(4):
                w, kc = i // 2, i % 2
                for r in range(KD):
                    last = pe.transpose(bank[i][:, r * P:(r + 1) * P], wqk1[:, w, r, kc * P:(kc + 1) * P], ident)
                last.then_inc(wT_pe, 1)
            pe.wait_ge(wv_in, 16 * 2)
            for k in range(KD):
                last = pe.transpose(bank[6][:, k * E:(k + 1) * E], gw_s[:, k * P:(k + 1) * P], ident[0:E, 0:E])
            last.then_inc(wT_pe, 1)
            pe.wait_ge(wT_ok, 4)
            for m in range(KD):
                for k in range(KD):
                    last = pe.matmul(bank[4 + m][:, 0:D], wqk1T[:, 0, k, m * P:(m + 1) * P], wqk1T[:, 1, k, :],
                                     start=(k == 0), stop=(k == KD - 1))
                last.then_inc(gram_pe, 1)

            def turn_rows(p):
                pe.wait_ge(xn1_ok, p + 1)
                if p >= 2:
                    pe.wait_ge(x1_ok, TPP * (p - 1))
                for k in range(KD):
                    for i in range(TPP):
                        last = pe.transpose(bank[k][:, i * P:(i + 1) * P], xn1[:, i, k * P:(k + 1) * P], ident)
                    last.then_inc(t1_pe, 1)

            def fold(p):
                pe.wait_ge(t1_act, p + 1)
                pe.wait_ge(t1_dve, p + 1)
                if p == 0:
                    pe.wait_ge(gram_ok, KD)
                    pe.wait_ge(wT_ok, 5)
                if p == FIRST_PROJECTED + 1:
                    pe.wait_ge(pj_dve, 4)
                for m in range(KD):
                    for k in range(KD):
                        last = pe.matmul(bank[2 + m], gram[:, k, m * P:(m + 1) * P], xT[:, k, :],
                                         start=(k == 0), stop=(k == KD - 1))
                    last.then_inc(u_pe, 1)

            def values1(p):
                for i in range(TPP):
                    for k in range(KD):
                        last = pe.matmul(bank[4 + i // 2][:, (i % 2) * D:(i % 2 + 1) * D],
                                         xT[:, k, i * P:(i + 1) * P], wv1_s[:, k, :],
                                         start=(k == 0), stop=(k == KD - 1), skip_group_check=True)
                    if i % 2:
                        last.then_inc(v_pe, 1)

            def scores1(p):
                pe.wait_ge(u_act, p + 1)
                pe.wait_ge(u_dve, p + 1)
                for i in range(2):
                    o = i * S
                    for k in range(KD):
                        pe.matmul(bank[6 + i][:, 0:S], xT[:, k, o:o + P], uT[:, k, o:o + S],
                                  start=(k == 0), stop=(k == KD - 1))
                    for k in range(KD):
                        last = pe.matmul(bank[6 + i][:, S:S + P], xT[:, k, o + P:o + S], uT[:, k, o + P:o + S],
                                         start=(k == 0), stop=(k == KD - 1))
                    last.then_inc(s1_pe, 1)

            def retain(p):
                pe.wait_ge(pr_ok, 4 * (p + 1))
                pe.wait_ge(v_act, p + 1)
                pe.wait_ge(v_dve, p + 1)
                for i in range(TPP):
                    b, q = i // 2, i % 2
                    dst = bank[i // 2][:, q * D:(q + 1) * D]
                    last = pe.matmul(dst, pr[:, b, q * P:(q + 1) * P], v1[:, 2 * b, :], start=True, stop=(q == 0))
                    if q == 1:
                        last = pe.matmul(dst, pr[:, b, 2 * P:3 * P], v1[:, 2 * b + 1, :], start=False, stop=True)
                    last.then_inc(o1_pe, 1)

            def project(p, i):
                if p >= 1:
                    if i == 9:
                        pe.wait_ge(pj_dve, 4 * p + 2)
                    elif i >= 1:
                        pe.wait_ge(pj_act, 8 * p + i)
                    else:
                        pe.wait_ge(pj_dve, 4 * p)
                    if i == 0 and p >= 2:
                        pe.wait_ge(m_ok, 2 * p - 2)
                    if i == 4:
                        pe.wait_ge(m_ok, 2 * p - 1)
                elif i >= 2:
                    pe.wait_ge(pj_act, i - 1)
                if i in (4, 6):
                    pe.wait_ge(pj_act, 8 * p + i - 2)
                if i < 4:
                    k = i % 2
                    if i == 0:
                        pe.wait_ge(xn2_ok, p + 1)
                    if i == 2:
                        pe.wait_ge(c_in[p], 16)
                    for t in range(TPP):
                        src = (xn2[:, p % 2, t, k * P:(k + 1) * P] if i < 2 else cx[:, t, k * P:(k + 1) * P])
                        last = pe.transpose(piece_bank(p, i)[:, t * P:(t + 1) * P], src, ident)
                elif i < 8:
                    which, g = (i - 4) // 2, i % 2
                    for k in range(KD):
                        last = pe.matmul(piece_bank(p, i), (wq_p, wk_p)[which][:, k, g].rearrange("p d h -> p (d h)"),
                                         (xT, cT)[which][:, k, :], start=(k == 0), stop=(k == KD - 1))
                else:
                    for j in range(2):
                        t = 2 * (i - 8) + j
                        for k in range(KD):
                            last = pe.matmul(piece_bank(p, i)[:, j * D:(j + 1) * D], cT[:, k, t * P:(t + 1) * P],
                                             wv_s[:, k, :], start=(k == 0), stop=(k == KD - 1), skip_group_check=True)
                last.then_inc(pj_pe, 1)

            def scores(b, u, j):
                n = 3 * (NU * b + u) + j
                p, o, dst = b // 2, (b % 2) * S, bank[n % 2]
                if n >= 2:
                    pe.wait_ge(s_max, n - 1)
                if n % (6 * NU) == 0:
                    pe.wait_ge(stack_in[p], STACKED)
                if j == 0:
                    pe.matmul(dst, ident_b[:], mask_b[:], start=True, stop=False, skip_group_check=True)
                    for i in range(U):
                        h = U * u + i
                        last = pe.matmul(dst[:, i * P:(i + 1) * P], qst[0:KS, p % 2, h, o:o + P],
                                         kst[0:KS, p % 2, h, o:o + P], start=False, stop=(i == U - 1),
                                         skip_group_check=True)
                else:
                    pe.matmul(dst.rearrange("p (h k) -> p h k", h=2)[:, :, P:S], ident_b[:],
                              mask_b[:, 0:S].rearrange("p (h k) -> p h k", h=2), start=True, stop=False,
                              skip_group_check=True)
                    for i in range(2):
                        h = U * u + 2 * (j - 1) + i
                        last = pe.matmul(dst[:, i * S:(i + 1) * S], qst[0:KS, p % 2, h, o + P:o + S],
                                         kst[0:KS, p % 2, h, o:o + S], start=False, stop=(i == 1),
                                         skip_group_check=True)
                last.then_inc(s_pe, 1)

            def maxima_turned(b):
                pe.wait_ge(s_max, 3 * NU * (b + 1))
                p, later = (b + 2) // 2, (b + 2) % 2
                if p >= PAIRS:
                    p, later = PAIRS - 1, 1
                pe.wait_ge(pj_act, 8 * p + (8 if later else 4))
                pe.wait_ge(pj_dve, 4 * p + 4 * later)
                if b >= 1:
                    pe.wait_ge(m_ok, b)
                for q in range(2):
                    last = pe.transpose(bank[7][0:H, q * P:(q + 1) * P], mx[:, b % 2, q, :], ident)
                last.then_inc(m_pe, 1)

            def shifted(b, u, j):
                n = 3 * (NU * b + u) + j
                p, o, dst = b // 2, (b % 2) * S, bank[2 + n % 2]
                if n >= 2:
                    pe.wait_ge(exp_ok, n - 1)
                if u == 0 and j == 0:
                    pe.wait_ge(max_in[b % 2], 32 * (b // 2 + 1))
                for i in range(U if j == 0 else 2):
                    if j == 0:
                        h = U * u + i
                        last = pe.matmul(dst[:, i * P:(i + 1) * P], kst[:, p % 2, h, o + P:o + S],
                                         qst[:, p % 2, h, o + P:o + S], start=True, stop=True)
                    else:
                        h = U * u + 2 * (j - 1) + i
                        last = pe.matmul(dst[:, i * S:(i + 1) * S], kst[:, p % 2, h, o:o + P],
                                         qst[:, p % 2, h, o:o + S], start=True, stop=True)
                last.then_inc(st_pe, 1)

            def weigh(b, u):
                n = NU * b + u
                pe.wait_ge(sel_ok, 3 * (n + 1))
                if n >= 1:
                    pe.wait_ge(ot_ok, n)
                if u == 0 and b % 2 == 0:
                    pe.wait_ge(pj_dve, 4 * (b // 2 + 1))
                for kt_ in range(2):
                    for i in range(U):
                        lhs = va[:, (b // 2) % 2, 2 * (b % 2) + kt_, U * u + i, :]
                        if kt_ == 0:
                            rhs = pT[:, (3 * n + 1 + i // 2) % 6, (i % 2) * S:(i % 2 + 1) * S]
                            dst = bank[4][VW * i:VW * (i + 1), 0:S]
                        else:
                            rhs = pT[:, (3 * n) % 6, i * P:(i + 1) * P]
                            dst = bank[4][VW * i:VW * (i + 1), P:S]
                        last = pe.matmul(dst, lhs, rhs, start=(kt_ == 0), stop=(kt_ == 1), skip_group_check=True)
                last.then_inc(pv_pe, 1)

            def visit(b, v):
                if v == 0:
                    pe.wait_ge(ot_ok, NU * (b + 1))
                    if b >= 1:
                        pe.wait_ge(slot_ok, b)
                    for q in range(2):
                        for u in range(NU):
                            last = pe.transpose(pair[:, q, u * P:(u + 1) * P], oT[:, b % 2, u, q * P:(q + 1) * P], ident)
                    last.then_inc(e1_pe, 1)
                if v == 1:
                    pe.wait_ge(on_ok, b + 1)
                    for q in range(2):
                        for k in range(KD):
                            last = pe.transpose(pair[:, q, k * P:(k + 1) * P], o_n[:, q, k * P:(k + 1) * P], ident)
                    last.then_inc(e2_pe, 1)
                if v == 2:
                    pe.wait_ge(oT2_ok, b + 1)
                    for q in range(2):
                        for k in range(KD):
                            last = pe.matmul(pair[:, q, 0:D], oT2[:, q, k, :], wo_s[:, k, :], start=(k == 0),
                                             stop=(k == KD - 1))
                    last.then_inc(e3_pe, 1)
                if v == 3:
                    pe.wait_ge(x3n_ok, b + 1)
                    for q in range(2):
                        for k in range(KD):
                            last = pe.transpose(pair[:, q, k * P:(k + 1) * P], x3n[:, q, k * P:(k + 1) * P], ident)
                    last.then_inc(e4_pe, 1)
                if v == 4:
                    pe.wait_ge(x3T_ok, b + 1)
                    for q in range(2):
                        for k in range(KD):
                            last = pe.matmul(pair[:, q, 0:E], x3T[:, q, k, :], gwT[:, k, :], start=(k == 0),
                                             stop=(k == KD - 1))
                    last.then_inc(e5_pe, 1)
                if v == 5:
                    pe.wait_ge(hot_ok, b + 1)
                    pe.wait_ge(gexp_ok, 2 * b + 2)
                    if b >= 1:
                        pe.wait_ge(seen_ok, b)
                    for q in range(2):
                        dst = pair[:, q, 32:32 + E]
                        pe.matmul(dst, before_b[:], hot[:, q, :], start=True, stop=False)
                        if q == 1:
                            pe.matmul(dst, ones_b[:], hot[:, 0, :], start=False, stop=False)
                        last = pe.matmul(dst, ones_b[:], seen[:, b % 2, :], start=False, stop=True)
                    last.then_inc(e6_pe, 1)

            for p in range(PAIRS):
                turn_rows(p)
                fold(p)
                if p >= 1:
                    retain(p - 1)
                values1(p)
                scores1(p)
                if p == FIRST_PROJECTED:
                    pe.wait_ge(perm_ok, 2 * KD * G)
                    for i in range(10):
                        project(0, i)
            retain(PAIRS - 1)
            pe.wait_ge(cast_ok, 6)
            pe.wait_ge(ones_ok, 4)
            pe.wait_ge(kone_in, 32)
            pe.wait_ge(x1_ok, NT)
            for T in STEPS:
                if scored_at(T):
                    b, k = scored_at(T)
                    scores(b, k // 3, k % 3)
                if weighed_at(T):
                    b, k = weighed_at(T)
                    shifted(b, k // 3, k % 3)
                for b, v in visits_at(T):
                    visit(b, v)
                if piece_at(T):
                    project(*piece_at(T))
                if sums_at(T) is not None:
                    weigh(*divmod(sums_at(T), NU))
                if scored_at(T) and scored_at(T)[1] == LAST:
                    maxima_turned(scored_at(T)[0])

            def turn_slots(e):
                pe.wait_ge(xdn_ok, e + 1)
                for k in range(KD):
                    for j in range(2):
                        last = pe.transpose(bank[0][:, k * CAP + j * HALF:k * CAP + (j + 1) * HALF],
                                            xdn[:, j, k * P:(k + 1) * P], ident[0:HALF, 0:HALF])
                last.then_inc(xdT_pe, 1)

            def hidden(e):
                pe.wait_ge(xdT_ok, e + 1)
                pe.wait_ge(w1_in[e % WR], 16 * (e // WR + 1))
                for f in range(FT):
                    for k in range(KD):
                        last = pe.matmul(bank[1 + f // 3][:, (f % 3) * CAP:(f % 3 + 1) * CAP],
                                         w1_s[e % WR][:, k, f * P:(f + 1) * P], xdT[:, k, :],
                                         start=(k == 0), stop=(k == KD - 1), skip_group_check=True)
                    if f % 3 == 2 or f == FT - 1:
                        last.then_inc(h_pe, 1)

            def back(e):
                pe.wait_ge(yT_ok, e + 1)
                if e >= 1:
                    pe.wait_ge(yo_ok, e)
                for j in range(2):
                    for k in range(KD):
                        last = pe.transpose(bank[5][0:HALF, j * D + k * P:j * D + (k + 1) * P],
                                            yT[:, k, j * HALF:(j + 1) * HALF], ident)
                last.then_inc(z_pe, 1)

            def outward(e):
                pe.wait_ge(w2_in[e % WR], 16 * (e // WR + 1))
                for k in range(KD):
                    for f in range(FT):
                        if k == 0 and f in (0, 6):
                            pe.wait_ge(h_act, 2 * e + 1 + (f == 6))
                        if k == 0 and f == 3:
                            pe.wait_ge(h_dve, e + 1)
                        last = pe.matmul(bank[4][:, k * CAP:(k + 1) * CAP], w2_s[e % WR][:, f, k * P:(k + 1) * P],
                                         hT[:, f, :], start=(f == 0), stop=(f == FT - 1), skip_group_check=True)
                last.then_inc(y_pe, 1)

            turn_slots(0)
            for e in range(E):
                hidden(e)
                if e >= 1:
                    back(e - 1)
                if e + 1 < E:
                    turn_slots(e + 1)
                outward(e)
            back(E - 1)


BANKS = 3 * NU
LAST = BANKS - 1
LEAD = 3
FIRST_PROJECTED = PAIRS - 2
NORM, APPLY = 6, 7
VISITS = {4: 0, 6: 1, 8: 2, 9: NORM, 10: APPLY, 11: 3, 13: 4, 15: 5}
STEPS = range((B + 1) * BANKS + LEAD + max(VISITS) + 1)


def scored_at(T):
    return divmod(T, BANKS) if T < B * BANKS else None


def weighed_at(T):
    t = T - BANKS - LEAD
    return divmod(t, BANKS) if 0 <= t < B * BANKS else None


def sums_at(T):
    t = T - BANKS - LEAD
    return t // 3 - 1 if t % 3 == 2 and 3 <= t < B * BANKS + 3 else None


def visits_at(T):
    t = T - 2 * BANKS - LEAD
    return [((t - o) // BANKS, v) for o, v in sorted(VISITS.items(), reverse=True)
            if (t - o) % BANKS == 0 and 0 <= (t - o) // BANKS < B]


def piece_at(T):
    p, r = divmod(T + 20, 2 * BANKS)
    return (p, r // 2) if 1 <= p < PAIRS and r % 2 == 0 and r < 20 else None


_INS = ['x', 'ctx_1024', 'L0_attn_weight_q', 'L0_attn_weight_k', 'L0_attn_weight_v', 'L0_attn_theta',
        'L0_xattn_wq', 'L0_xattn_bq', 'L0_xattn_wk', 'L0_xattn_bk', 'L0_xattn_wv', 'L0_xattn_bv',
        'L0_xattn_wo', 'L0_xattn_bo', 'L0_ffn_gate_w', 'L0_ffn_w1', 'L0_ffn_w2']


def constants():
    import numpy as np
    r, c = np.arange(P)[:, None], np.arange(P)[None, :]
    q = np.arange(2 * P)[None, :]
    decay = np.where(q >= r, np.float32(0.96875) ** np.maximum(q - r, 0).astype(np.float32), 0)
    return np.concatenate([
        np.eye(P), decay, np.where(c > r, NEG, 0), (r < c), np.broadcast_to(np.arange(E)[None, :], (P, E)),
        r + P * np.arange(NT)[None, :]], axis=1).astype(np.float32)


def kernel(**inputs):
    import numpy as _np
    import concourse.bacc as _bacc
    from concourse import mybir as _mybir
    from concourse.bass_utils import run_bass_kernel_spmd as _run

    nc = _bacc.Bacc("TRN2", target_bir_lowering=False, num_devices=1)
    arrays, args = {}, []
    for name, a in [(n, inputs[n]) for n in _INS] + [("constants", constants())]:
        a = _np.ascontiguousarray(a)
        arrays[f"in_{name}_dram"] = a
        args.append(nc.dram_tensor(f"in_{name}_dram", a.shape, _mybir.dt.from_np(a.dtype), kind="ExternalInput").ap())
    out = nc.dram_tensor("out_0_dram", (B, S, D), _mybir.dt.float32, kind="ExternalOutput").ap()
    decoder_layer(nc, *args, out)
    r = _run(nc, [arrays], core_ids=[0])
    return r.results[0]["out_0_dram"]
```

```python
from contextlib import ExitStack

import concourse.bass as bass
from concourse import mybir

ALU = mybir.AluOpType
ACT = mybir.ActivationFunctionType
AX = mybir.AxisListType.X
F32 = mybir.dt.float32
BF16 = mybir.dt.bfloat16
F32R = mybir.dt.float32r
U32 = mybir.dt.uint32

P = 128
B, S, D = 8, 256, 256
KD = D // P
TOK = B * S
NT = TOK // P
PAIRS = B // 2
PT = 2 * S
TPP = PT // P
H, DH = 16, 16
HG = P // DH
G = H // HG
STACKED = 16 * 2 * G * 6
U = 4
NU = H // U
PARTS = 3
PASSES = ((0, 0), (1, 0), (0, 1))
COMBOS = ((0, 0), (0, 1), (1, 0), (1, 1), (0, 2), (2, 0))
KS = len(COMBOS) * DH
KM = KS + 2
VW = 32
E, F = 16, 1024
FT = F // P
CAP = int(1.25 * TOK / E)
HALF = CAP // 2
SLOTS = E * CAP
REC = D + 4
FAR = float(1 << 20)
EPS = 1e-5
NEG = -1e30
WR = 4

C_ID, C_DECAY, C_MASK, C_BEFORE, C_IOTA, C_TOK = 0, 128, 384, 512, 640, 656
C_END = C_TOK + NT


def decoder_layer(nc, x, ctx_in, wq1, wk1, wv1, theta, wq, bq, wk, bk, wv, bv, wo, bo,
                  gate_w, w1, w2, consts, out):
    slots = nc.dram_tensor("slots", (SLOTS, REC), F32, kind="Internal").ap()
    x_v = x.rearrange("b s d -> (b s) d").rearrange("(t p) d -> p t d", p=P)
    ctx_v = ctx_in.rearrange("b s d -> (b s) d").rearrange("(t p) d -> p t d", p=P)
    out_rows = out.rearrange("b s d -> (b s) d")

    with ExitStack() as stack:
        def sb(name, shape, dt=F32):
            return stack.enter_context(nc.sbuf_tensor(name, shape, dt))

        def sem(name):
            return stack.enter_context(nc.semaphore(name))

        bank = [stack.enter_context(nc.psum_tensor(f"bank{i}", [P, 512], F32))[:] for i in range(8)]
        pair = bank[5].rearrange("p (q c) -> p q c", q=2)

        SCORE_BANK = (bank[0], bank[1], bank[6])
        cst = sb("cst", [P, C_END])
        ident = cst[:, C_ID:C_ID + P]
        decay = cst[:, C_DECAY:C_DECAY + 2 * P]
        iota_e = cst[:, C_IOTA:C_IOTA + E]
        ident_b = sb("ident_b", [P, P], BF16)
        mask_b = sb("mask_b", [P, 4 * P], BF16)
        before_b = sb("before_b", [P, P], BF16)
        ones_b = sb("ones_b", [P, P], BF16)
        wq_s = sb("wq_s", [P, KD, D])
        wk_s = sb("wk_s", [P, KD, D])
        wv_s = sb("wv_s", [P, KD, D])
        wo_s = sb("wo_s", [P, KD, D])
        wq_p = sb("wq_p", [P, KD, G, DH, HG])
        wk_p = sb("wk_p", [P, KD, G, DH, HG])
        gw_s = sb("gw_s", [E, D])
        gwT = sb("gwT", [P, KD, E])
        cols = sb("cols", [P, 3, KD])
        turn = sb("turn", [P, KD])
        bv_s = sb("bv_s", [P, D])
        bo_s = sb("bo_s", [P, D])

        def carver(name, words):
            region, at = sb(name, [P, words]), [0]

            def cut(shape, dt=F32, rows=P):
                size = 1
                for n in shape:
                    size *= n
                size = size // 2 if dt == BF16 else size
                view = region[0:rows, at[0]:at[0] + size]
                at[0] += size
                assert at[0] <= words
                if dt != F32:
                    view = view.bitcast(dt)
                names = [f"a{i}" for i in range(len(shape))]
                sizes = {n: m for n, m in zip(names[1:], shape[1:])}
                return view.rearrange(f"p ({' '.join(names)}) -> p {' '.join(names)}", **sizes)

            def again(word):
                at[0] = word
            return cut, again

        cut, again = carver("region_q", 2 * H * PT // 2)
        qst = cut([2, H, PT], BF16, KM)
        again(H * PT // 2)
        xn1 = cut([TPP, D])
        uT = cut([KD, PT])
        v1 = cut([TPP, D])
        pr = cut([2, 3 * P])
        again(0)
        xd = cut([3, 2, REC], F32, HALF)
        xdn = cut([2, D], F32, HALF)
        xdT = cut([KD, CAP])
        hT = cut([FT, CAP])
        yT = cut([KD, CAP])
        yo = cut([2, 2, D], F32, HALF)
        cut, again = carver("region_k", 2 * H * PT // 2)
        kst = cut([2, H, PT], BF16, KM)
        again(0)
        w_slot2 = (cut([KD, F]), cut([FT, D]))
        w_slot3 = (cut([KD, F]), cut([FT, D]))
        cut, again = carver("region_v", 2 * TPP * H * VW)
        va = cut([2, TPP, H, VW])
        again(0)
        w_slot1 = (cut([KD, F]), cut([FT, D]))
        cut, again = carver("region_w", KD * F + FT * D)
        wqk1 = cut([2, KD, D])
        wqk1T = cut([2, KD, D])
        wv1_s = cut([KD, D])
        again(0)
        w_slot0 = (cut([KD, F]), cut([FT, D]))
        w1_s, w2_s = zip(w_slot0, w_slot1, w_slot2, w_slot3)

        xs = sb("xs", [P, NT, D])
        cx = sb("cx", [P, TPP, D])
        stats = sb("stats", [P, TPP, 6])
        mv = sb("mv", [P, 2, NT, 2])
        rstd = sb("rstd", [P, 2, NT])
        vare = sb("vare", [P, TPP])
        mhalf = sb("mhalf", [P, TPP])
        xn2 = sb("xn2", [P, 2, TPP, D])
        xT = sb("xT", [P, KD, PT])
        cT = sb("cT", [P, KD, PT])
        qk = sb("qk", [P, G, PT])
        parts = sb("parts", [P, 2, G, PARTS, PT], BF16)
        mx = sb("mx", [P, 2, 2, H])
        mrow = sb("mrow", [H, 2, S], BF16)
        with ExitStack() as early:
            def pair_of_parts(name, width):
                return tuple(early.enter_context(nc.sbuf_tensor(f"{name}_{part}", [P, KD, width], F32R))[:]
                             for part in ("high", "low"))
            xT_parts = pair_of_parts("xT", PT)
            gram_parts = pair_of_parts("gram", D)
            wv1_parts = pair_of_parts("wv1", D)
        pT = sb("pT", [P, 6, 512])
        oT = sb("oT", [P, 2, NU, S])
        rden = sb("rden", [P, 2, H])
        o_n = sb("o_n", [P, 2, D])
        oT2 = sb("oT2", [P, 2, KD, P])
        rec = sb("rec", [P, 2, 2, REC])
        st3 = sb("st3", [P, 2, 6])
        var3 = sb("var3", [P, 2, 1])
        x3n = sb("x3n", [P, 2, D])
        x3T = sb("x3T", [P, 2, KD, P])
        top = sb("top", [P, 2, 8])
        topi = sb("topi", [P, 2, 8], U32)
        gsm = sb("gsm", [P, 6, 2])
        gexp = sb("gexp", [P, 2, E])
        hot = sb("hot", [P, 2, E], BF16)
        ahead = sb("ahead", [P, 2, E])
        seen = sb("seen", [P, 2, E], BF16)
        slot_u = sb("slot_u", [P, NT], U32)
        blank = sb("blank", [P, REC])

        cst_in, wa_in, wb_in, sm_in = sem("cst_in"), sem("wa_in"), sem("wb_in"), sem("sm_in")
        x_in = [sem(f"x_in{p}") for p in range(PAIRS)]
        c_in = [sem(f"c_in{p}") for p in range(PAIRS)]
        stack_in = [sem(f"stack_in{i}") for i in range(4)]
        max_in = [sem(f"max_in{i}") for i in range(2)]
        blank_out, row_out = sem("blank_out"), [sem(f"row_out{i}") for i in range(2)]
        scattered = [sem(f"scattered{i}") for i in range(2)]
        w1_in = [sem(f"w1_in{i}") for i in range(WR)]
        w2_in = [sem(f"w2_in{i}") for i in range(WR)]
        xd_in = [sem(f"xd_in{i}") for i in range(3)]
        final_out = [sem(f"final_out{i}") for i in range(2)]
        id_in, wv_in, th_in = sem("id_in"), sem("wv_in"), sem("th_in")
        blank_ok, half_ok, ones_ok, cast_ok, turn_ok = (sem("blank_ok"), sem("half_ok"), sem("ones_ok"),
                                                        sem("cast_ok"), sem("turn_ok"))
        wT_pe, wT_ok, gram_pe, gram_ok = sem("wT_pe"), sem("wT_ok"), sem("gram_pe"), sem("gram_ok")
        dve_c, pool_c, act_c = sem("dve_c"), sem("pool_c"), sem("act_c")
        stat1, rstd1, xn1_ok = sem("stat1"), sem("rstd1"), sem("xn1_ok")
        stat2, rstd2, xn2_ok = sem("stat2"), sem("rstd2"), sem("xn2_ok")
        t1_pe, whole1_ok, high1_ok, low1_ok = sem("t1_pe"), sem("whole1_ok"), sem("high1_ok"), sem("low1_ok")
        gram_low_ok, wv1_high_ok, wv1_low_ok = sem("gram_low_ok"), sem("wv1_high_ok"), sem("wv1_low_ok")
        u_pe, u_act, u_dve = sem("u_pe"), sem("u_act"), sem("u_dve")
        v_pe, v_act, v_dve = sem("v_pe"), sem("v_act"), sem("v_dve")
        s1_pe, pr_ok, o1_pe, x1_ok, xb_ok = sem("s1_pe"), sem("pr_ok"), sem("o1_pe"), sem("x1_ok"), sem("xb_ok")
        pj_pe, pj_act, pj_dve, split_ok = sem("pj_pe"), sem("pj_act"), sem("pj_dve"), sem("split_ok")
        rest_ok = sem("rest_ok")
        s_pe, s_max, m_pe, m_ok = sem("s_pe"), sem("s_max"), sem("m_pe"), sem("m_ok")
        st_pe, exp_ok, sel_ok, pv_pe, ot_ok = sem("st_pe"), sem("exp_ok"), sem("sel_ok"), sem("pv_pe"), sem("ot_ok")
        e1_pe, on_ok, e2_pe, oT2_ok, e3_pe, x3_ok = (sem("e1_pe"), sem("on_ok"), sem("e2_pe"), sem("oT2_ok"),
                                                     sem("e3_pe"), sem("x3_ok"))
        rstd3, x3n_ok, e4_pe, x3T_ok, e5_pe = sem("rstd3"), sem("x3n_ok"), sem("e4_pe"), sem("x3T_ok"), sem("e5_pe")
        seen_ok, kone_in, perm_ok = sem("seen_ok"), sem("kone_in"), sem("perm_ok")
        hot_ok, gexp_ok, e6_pe, slot_ok = sem("hot_ok"), sem("gexp_ok"), sem("e6_pe"), sem("slot_ok")
        xdn_ok, xdT_pe, xdT_ok = sem("xdn_ok"), sem("xdT_pe"), sem("xdT_ok")
        h_pe, h_act, h_dve, y_pe, yT_ok = sem("h_pe"), sem("h_act"), sem("h_dve"), sem("y_pe"), sem("yT_ok")
        z_pe, yo_ok = sem("z_pe"), sem("yo_ok")

        block = stack.enter_context(nc.Block())

        def piece_bank(p, i):
            return bank[7] if p else bank[2 + i % 2]

        def kt(w):
            return w.rearrange("(k p) n -> p k n", p=P)

        @block.sync
        def _(sp):
            sp.dma_start(xs[:, 0:TPP, :], x_v[:, 0:TPP, :]).then_inc(x_in[0], 16)
            sp.dma_start(wqk1[:, 1], kt(wk1)).then_inc(wa_in, 16)
            sp.dma_start(cst[:, C_DECAY:C_END], consts[:, C_DECAY:C_END]).then_inc(cst_in, 16)
            sp.dma_start(wv1_s[:], kt(wv1)).then_inc(wv_in, 16)
            sp.dma_start(gw_s[:], gate_w).then_inc(wv_in, 16)
            with nc.allow_non_contiguous_dma(reason="256 numbers, one a partition"):
                for i, w in ((1, bq), (2, bk)):
                    for g in range(G):
                        sp.dma_start(cols[:, i, g:g + 1], w[g * P:(g + 1) * P].rearrange("(h d) -> d h", h=HG)
                                     ).then_inc(sm_in, 16)
            for p in range(1, PAIRS):
                sp.dma_start(xs[:, TPP * p:TPP * (p + 1), :], x_v[:, TPP * p:TPP * (p + 1), :]).then_inc(x_in[p], 16)
            for w_s, w in ((wq_s, wq), (wk_s, wk), (wv_s, wv), (wo_s, wo)):
                sp.dma_start(w_s[:], kt(w)).then_inc(wb_in, 16)
            sp.dma_start(bv_s[:], bv.rearrange("(a n) -> a n", a=1).to_broadcast((P, D))).then_inc(wb_in, 16)
            sp.dma_start(bo_s[:], bo.rearrange("(a n) -> a n", a=1).to_broadcast((P, D))).then_inc(wb_in, 16)
            sp.dma_start(cx[:], ctx_v[:, 0:TPP, :]).then_inc(c_in[0], 16)
            sp.wait_ge(ones_ok, 1)
            for r in range(2):
                sp.dma_start(kst[KS + r:KS + r + 1].rearrange("r a h t -> r (a h t)"), ones_b[:]).then_inc(kone_in, 16)
            sp.wait_ge(blank_ok, 2)
            sp.dma_start(slots.rearrange("(p j) r -> p j r", p=P),
                         blank[:].rearrange("p (a r) -> p a r", a=1).to_broadcast((P, SLOTS // P, REC))
                         ).then_inc(blank_out, 16)

            def load_w(e):
                s = e % WR
                if e == 1:
                    sp.wait_ge(pv_pe, NU * B)
                elif e in (2, 3):
                    sp.wait_ge(st_pe, 3 * NU * B)
                elif e >= WR:
                    sp.wait_ge(h_pe, 3 * (e - WR + 1))
                sp.dma_start(w1_s[s], w1[e].rearrange("(k p) f -> p k f", p=P)).then_inc(w1_in[s], 16)
                if e >= WR:
                    sp.wait_ge(y_pe, e - WR + 1)
                sp.dma_start(w2_s[s], w2[e].rearrange("(j p) d -> p j d", p=P)).then_inc(w2_in[s], 16)

            def project(p, i):
                if i == 4 and p + 1 < PAIRS:
                    sp.wait_ge(pj_pe, 10 * p + 4)
                    sp.dma_start(cx[:], ctx_v[:, TPP * (p + 1):TPP * (p + 2), :]).then_inc(c_in[p + 1], 16)
                if 5 <= i <= 8:
                    which, g = (i - 5) // 2, (i - 5) % 2
                    sp.wait_ge(split_ok, (2 * p + which) * G + g + 1)
                    if i == 5 and p >= 2:
                        sp.wait_ge(st_pe, 3 * NU * 2 * (p - 1))
                    for c, combo in enumerate(COMBOS):
                        dst = (qst, kst)[which][c * DH:(c + 1) * DH, p % 2, g * HG:(g + 1) * HG, :]
                        sp.dma_start(dst, parts[:, which, g, combo[which], :]
                                     ).then_inc(stack_in[p], 16)

            def max_rows(b):
                sp.wait_ge(m_ok, b + 1)
                for r in range(2):
                    sp.dma_start(qst[KS + r:KS + r + 1, (b // 2) % 2, :, (b % 2) * S:(b % 2 + 1) * S], mrow[:, r, :]
                                 ).then_inc(max_in[b % 2], 16)

            def visit(b, v):
                if v == 3:
                    sp.wait_ge(x3_ok, b + 1)
                    sp.dma_start(out_rows[b * S:(b + 1) * S, :].rearrange("(q p) d -> p q d", p=P), rec[:, b % 2, :, 0:D]
                                 ).then_inc(row_out[b % 2], 16)

            for i in range(10):
                project(0, i)
            sp.wait_ge(o1_pe, NT)
            load_w(0)
            for T in STEPS:
                for b, v in visits_at(T, SP_VISITS):
                    visit(b, v)
                if turned_at(T) is not None:
                    max_rows(turned_at(T))
                if piece_at(T):
                    project(*piece_at(T))
            load_w(1)
            for i in range(2):
                sp.wait_ge(scattered[i], 16 * 2 * (B // 2))

            def load_x(e):
                if e >= 3:
                    sp.wait_ge(final_out[(e - 3) % 2], 32 * ((e - 3) // 2 + 1))
                sp.dma_start(xd[:, e % 3], slots[e * CAP:(e + 1) * CAP, :].rearrange("(j p) r -> p j r", p=HALF)
                             ).then_inc(xd_in[e % 3], 16)
            for e in range(3):
                load_x(e)
            load_w(2)
            load_w(3)
            for e in range(E):
                if e + WR < E:
                    load_w(e + WR)
                if e + 3 < E:
                    load_x(e + 3)

        @block.gpsimd
        def _(pool):
            chain = [0]

            def link(ins):
                chain[0] += 1
                ins.then_inc(pool_c, 1)
                pool.wait_ge(pool_c, chain[0])

            pool.memset(blank[:, 0:D + 3], 0.0).then_inc(blank_ok, 1)
            pool.memset(blank[:, D + 3:REC].bitcast(U32), int(FAR)).then_inc(blank_ok, 1)
            pool.memset(mhalf[:], -0.5).then_inc(half_ok, 1)
            pool.memset(ones_b[:], 1.0).then_inc(ones_ok, 1)
            pool.memset(seen[:, 0, :], 0.0).then_inc(ones_ok, 1)
            pool.wait_ge(half_ok, 1)

            def reciprocal_deviation(dst, var, n):
                link(pool.tensor_scalar(vare[:, 0:n], var, EPS, None, ALU.add))
                return pool.tensor_tensor(dst, vare[:, 0:n], mhalf[:, 0:n], ALU.pow)

            def norm1(p):
                pool.wait_ge(stat1, TPP * (p + 1))
                reciprocal_deviation(rstd[:, 0, TPP * p:TPP * (p + 1)], mv[:, 0, TPP * p:TPP * (p + 1), 1], TPP
                                     ).then_inc(rstd1, 1)
                pool.wait_ge(rstd1, p + 1)

            def norm2(p):
                pool.wait_ge(stat2, TPP * (p + 1))
                reciprocal_deviation(rstd[:, 1, TPP * p:TPP * (p + 1)], mv[:, 1, TPP * p:TPP * (p + 1), 1], TPP
                                     ).then_inc(rstd2, 1)
                pool.wait_ge(rstd2, p + 1)

            def bias_residual(p):
                for i in range(TPP):
                    bias_tile(p, i)

            def bias_tile(p, i):
                pool.wait_ge(xn2_ok, TPP * p + i + 1)
                pool.tensor_tensor(xs[:, TPP * p + i, :], xs[:, TPP * p + i, :], bo_s[:], ALU.add
                                       ).then_inc(xb_ok, 1)

            norm1(0)
            pool.wait_ge(wv_in, 16 * 2)
            pool.wait_ge(wv1_high_ok, 1)
            pool.tensor_tensor(wv1_parts[1], wv1_s[:], wv1_parts[0].bitcast(F32), ALU.subtract).then_inc(wv1_low_ok, 1)
            va_heads = va.rearrange("p a t h w -> p (a t h) w")
            pool.memset(va_heads[:, :, DH + 1:VW], 0.0).then_inc(ones_ok, 1)
            pool.memset(va_heads[:, :, DH:DH + 1], 1.0).then_inc(ones_ok, 1)

            def retention(p):
                for k in range(KD):
                    pool.wait_ge(low1_ok, 2 * p + k + 1)
                    pool.tensor_tensor(xT[:, k, :], xT_parts[0][:, k, :].bitcast(F32),
                                       xT_parts[1][:, k, :].bitcast(F32), ALU.add).then_inc(whole1_ok, 1)
                if p + 1 < PAIRS:
                    norm1(p + 1)
                if p >= 1:
                    norm2(p - 1)
                if p == 0:
                    pool.wait_ge(wb_in, 16 * 6)
                    for w_to, w_of in ((wq_p, wq_s), (wk_p, wk_s)):
                        for k in range(KD):
                            for g in range(G):
                                pool.tensor_copy(w_to[:, k, g], w_of[:, k, g * P:(g + 1) * P].rearrange(
                                    "p (h d) -> p d h", h=HG)).then_inc(perm_ok, 1)
                if 1 <= p <= 2:
                    bias_residual(p - 1)

            def project(p, i):
                if 5 <= i <= 8:
                    which, g = (i - 5) // 2, (i - 5) % 2
                    n = (2 * p + which) * G + g
                    pool.wait_ge(pj_act, 8 * p + 4 + 2 * which + g + 1)
                    pool.tensor_tensor(qk[:, g, :], qk[:, g, :], parts[:, which, g, 0, :], ALU.subtract
                                       ).then_inc(rest_ok, 1)

            def select(b, u, j):
                n = 3 * (NU * b + u) + j
                pool.wait_ge(exp_ok, n + 1)
                heads = U if j == 0 else 2
                view = pT[:, n % 6, :].rearrange("p (h q) -> p h q", h=heads)[:, :, 0:P]
                pool.affine_select(out=view, in_=view, compare_op=ALU.is_ge, fill=0.0, base=0,
                                   pattern=[[0, heads], [1, P]], channel_multiplier=-1).then_inc(sel_ok, 1)

            def norm3(b):
                pool.wait_ge(x3_ok, b + 1)
                link(pool.tensor_scalar(var3[:], rec[:, b % 2, :, D + 1:D + 2], EPS, None, ALU.add))
                pool.tensor_tensor(rec[:, b % 2, :, D + 1:D + 2], var3[:],
                                   mhalf[:, 0:2].rearrange("p (q a) -> p q a", a=1), ALU.pow).then_inc(rstd3, 1)

            def scatter(b):
                pool.wait_ge(slot_ok, b + 1)
                if b == 0:
                    pool.wait_ge(blank_out, 16)
                for q in range(2):
                    t = 2 * b + q
                    pool.indirect_dma_start(
                        out=slots, out_offset=bass.IndirectOffsetOnAxis(ap=slot_u[:, t:t + 1], axis=0),
                        in_=rec[:, b % 2, q, :], in_offset=None, bounds_check=SLOTS - 1, oob_is_err=False
                    ).then_inc(scattered[b % 2], 16)

            for p in range(PAIRS):
                retention(p)
                if p == FIRST_PROJECTED:
                    for i in range(10):
                        project(0, i)
            norm2(PAIRS - 1)
            for T in STEPS:
                for b, v in visits_at(T, POOL_VISITS):
                    if v == NORM:
                        norm3(b)
                    if v == 5:
                        scatter(b)
                if piece_at(T):
                    project(*piece_at(T))
                if rows_at(T - 1):
                    bias_tile(*rows_at(T - 1))
                if weighed_at(T):
                    b, k = weighed_at(T)
                    select(b, k // 3, k % 3)

            for i in range(2):
                pool.wait_ge(row_out[i], 16 * (B // 2))
            for e in range(E):
                pool.wait_ge(yo_ok, e + 1)
                for j in range(2):
                    pool.indirect_dma_start(
                        out=out_rows, out_offset=bass.IndirectOffsetOnAxis(
                            ap=xd[:, e % 3, j, D + 3:REC].bitcast(U32), axis=0),
                        in_=yo[:, e % 2, j, :], in_offset=None, bounds_check=TOK - 1, oob_is_err=False
                    ).then_inc(final_out[e % 2], 16)
            pool.wait_ge(final_out[0], 32 * (E // 2))
            pool.wait_ge(final_out[1], 32 * (E // 2))

        @block.scalar
        def _(act):
            chain = [0]

            def link(ins):
                chain[0] += 1
                ins.then_inc(act_c, 1)
                act.wait_ge(act_c, chain[0])

            def copy(dst, src):
                return act.activation(dst, src, ACT.Copy)

            act.dma_start(cst[:, 0:P], consts[:, 0:P]).then_inc(id_in, 16)
            act.dma_start(wqk1[:, 0], kt(wq1)).then_inc(wa_in, 16)
            with nc.allow_non_contiguous_dma(reason="256 numbers, one a partition"):
                act.dma_start(cols[:, 0, :], theta.rearrange("(k p) -> p k", p=P)).then_inc(th_in, 16)
            act.wait_ge(th_in, 16)
            act.activation(turn[:], cols[:, 0, :], ACT.Exp, scale=0.0).then_inc(turn_ok, 1)
            act.wait_ge(wv_in, 16 * 2)
            copy(wv1_parts[0], wv1_s[:]).then_inc(wv1_high_ok, 1)

            def retention(p):
                act.wait_ge(t1_pe, 2 * p + 1)
                copy(xT_parts[0][:, 0, :], bank[0]).then_inc(high1_ok, 1)
                act.wait_ge(t1_pe, 2 * p + 2)
                copy(xT_parts[0][:, 1, :], bank[1]).then_inc(high1_ok, 1)
                if p == 0:
                    for g in range(KD):
                        act.wait_ge(gram_pe, g + 1)
                        copy(gram_parts[0][:, g, :], bank[4 + g][:, 0:D]).then_inc(gram_ok, 1)
                act.wait_ge(u_pe, 2 * p + 1)
                copy(uT[:, 0, :], bank[0]).then_inc(u_act, 1)
                act.wait_ge(v_pe, 2 * p + 1)
                copy(v1[:, 0:2, :].rearrange("p t d -> p (t d)"), bank[4]).then_inc(v_act, 1)

            def project(p, i):
                if i >= 8:
                    return
                act.wait_ge(pj_pe, 10 * p + i + 1)
                if i < 4:
                    dst = (xT, cT)[i // 2][:, i % 2, :]
                    copy(dst, piece_bank(p, i)).then_inc(pj_act, 1)
                else:
                    which, g = (i - 4) // 2, i % 2
                    n = (2 * p + which) * G + g
                    if n >= G:
                        act.wait_ge(split_ok, n - G + 1)
                    if p >= 1:
                        act.wait_ge(stack_in[p - 1], STACKED)
                    if p == 0 and i == 4:
                        act.wait_ge(sm_in, 16 * 2 * G)
                    link(act.activation(qk[:, g, :], piece_bank(p, i), ACT.Identity,
                                        bias=cols[:, 1 + which, g:g + 1]))
                    act.activation(parts[:, which, g, 0, :], piece_bank(p, i), ACT.Identity,
                                   bias=cols[:, 1 + which, g:g + 1]).then_inc(pj_act, 1)

            def exps(b, u, j):
                n = 3 * (NU * b + u) + j
                act.wait_ge(st_pe, n + 1)
                if n >= 6:
                    act.wait_ge(pv_pe, (n - 6) // 3 + 1)
                act.activation(pT[:, n % 6, :], bank[2 + n % 2], ACT.Exp, scale=1.0 / D ** 0.5).then_inc(exp_ok, 1)

            def heads_out(b, u):
                n = NU * b + u
                act.wait_ge(pv_pe, n + 1)
                if b >= 2:
                    act.wait_ge(e1_pe, 2 * (b - 1))
                copy(oT[:, b % 2, u, :], bank[4][:, 0:S]).then_inc(ot_ok, 1)

            def visit(b, v):
                if v == 1:
                    act.wait_ge(e2_pe, b + 1)
                    copy(oT2[:].rearrange("p q k t -> p q (k t)"), pair[:, :, 0:D]).then_inc(oT2_ok, 1)
                if v == 3:
                    act.wait_ge(e4_pe, b + 1)
                    copy(x3T[:].rearrange("p q k t -> p q (k t)"), pair[:, :, 0:D]).then_inc(x3T_ok, 1)
                if v == 4:
                    act.wait_ge(hot_ok, b + 1)
                    for q in range(2):
                        act.activation(gexp[:, q, :], pair[:, q, 0:E], ACT.Exp, bias=gsm[:, 1, q:q + 1],
                                       accum_out=gsm[:, 2, q:q + 1]).then_inc(gexp_ok, 1)

            for p in range(PAIRS):
                retention(p)
                if p == FIRST_PROJECTED:
                    for i in range(10):
                        project(0, i)
            for T in STEPS:
                if sums_at(T - 1) is not None:
                    heads_out(*divmod(sums_at(T - 1), NU))
                if weighed_at(T):
                    b, k = weighed_at(T)
                    exps(b, k // 3, k % 3)
                if piece_at(T):
                    project(*piece_at(T))
                for b, v in visits_at(T, ACT_VISITS):
                    visit(b, v)

            def turned(e):
                act.wait_ge(xdT_pe, e + 1)
                copy(xdT.rearrange("p k c -> p (k c)"), bank[0][:, 0:KD * CAP]).then_inc(xdT_ok, 1)

            turned(0)
            for e in range(E):
                for i in (0, 2):
                    act.wait_ge(h_pe, 3 * e + i + 1)
                    n = 3 if i == 0 else 2
                    act.activation(hT[:, 3 * i:3 * i + n, :].rearrange("p f c -> p (f c)"),
                                   bank[1 + i][:, 0:n * CAP], ACT.Relu).then_inc(h_act, 1)
                if e + 1 < E:
                    turned(e + 1)
                act.wait_ge(y_pe, e + 1)
                copy(yT.rearrange("p k c -> p (k c)"), bank[4][:, 0:KD * CAP]).then_inc(yT_ok, 1)

        @block.vector
        def _(dve):
            chain = [0]

            def link(ins):
                chain[0] += 1
                ins.then_inc(dve_c, 1)
                dve.wait_ge(dve_c, chain[0])

            def stats1(p):
                dve.wait_ge(x_in[p], 16)
                for i in range(TPP):
                    dve.bn_stats(stats[:, i, :], xs[:, TPP * p + i, :]).then_inc(dve_c, 1)
                chain[0] += TPP
                dve.wait_ge(dve_c, chain[0])
                for i in range(TPP):
                    dve.bn_aggr(mv[:, 0, TPP * p + i, :], stats[:, i, :]).then_inc(stat1, 1)
                dve.wait_ge(stat1, TPP * (p + 1))

            def apply1(p):
                dve.wait_ge(rstd1, p + 1)
                for i in range(TPP):
                    t = TPP * p + i
                    last = dve.tensor_scalar(xn1[:, i, :], xs[:, t, :], mv[:, 0, t, 0:1], rstd[:, 0, t:t + 1],
                                             ALU.subtract, ALU.mult)
                last.then_inc(xn1_ok, 1)

            def stats2(p):
                for i in range(TPP):
                    dve.bn_stats(stats[:, i, :], xs[:, TPP * p + i, :]).then_inc(dve_c, 1)
                chain[0] += TPP
                dve.wait_ge(dve_c, chain[0])
                for i in range(TPP):
                    dve.bn_aggr(mv[:, 1, TPP * p + i, :], stats[:, i, :]).then_inc(stat2, 1)
                dve.wait_ge(stat2, TPP * (p + 1))

            def apply2(p, i):
                dve.wait_ge(rstd2, p + 1)
                if p >= 2:
                    dve.wait_ge(pj_pe, 10 * (p - 2) + 2)
                t = TPP * p + i
                dve.tensor_scalar(xn2[:, p % 2, i, :], xs[:, t, :], mv[:, 1, t, 0:1], rstd[:, 1, t:t + 1],
                                  ALU.subtract, ALU.mult).then_inc(xn2_ok, 1)

            stats1(0)
            dve.wait_ge(cst_in, 16)
            dve.wait_ge(id_in, 16)
            dve.tensor_copy(ident_b[:], ident).then_inc(cast_ok, 1)
            dve.tensor_copy(before_b[:], cst[:, C_BEFORE:C_BEFORE + P]).then_inc(cast_ok, 1)
            for i in range(4):
                dve.tensor_copy(mask_b[:, i * P:(i + 1) * P], cst[:, C_MASK:C_MASK + P]).then_inc(cast_ok, 1)
            apply1(0)
            dve.wait_ge(turn_ok, 1)
            for i in range(4):
                dve.wait_ge(wT_pe, i + 1)
                dve.tensor_scalar(wqk1T[:, i // 2, i % 2, :], bank[4 + i][:, 0:D], turn[:, i % 2:i % 2 + 1], None,
                                  ALU.mult).then_inc(wT_ok, 1)
            dve.wait_ge(wT_pe, 5)
            dve.tensor_copy(gwT[:].rearrange("p k e -> p (k e)"), bank[2][:, 0:KD * E]).then_inc(wT_ok, 1)

            def residual1(p):
                for i in range(TPP):
                    dve.wait_ge(o1_pe, TPP * p + 2 * (i // 2) + 2)
                    t = TPP * p + i
                    dve.tensor_tensor(xs[:, t, :], xs[:, t, :], bank[2 + i // 2][:, (i % 2) * D:(i % 2 + 1) * D],
                                      ALU.add).then_inc(x1_ok, 1)
                dve.wait_ge(x1_ok, TPP * (p + 1))

            def decayed(p):
                for i in range(2):
                    dve.wait_ge(s1_pe, 2 * p + i + 1)
                    dve.tensor_tensor(pr[:, i, 0:2 * P], bank[6 + i][:, 0:2 * P], decay, ALU.mult).then_inc(pr_ok, 1)
                    dve.tensor_tensor(pr[:, i, 2 * P:3 * P], bank[6 + i][:, 2 * P:3 * P], decay[:, 0:P],
                                      ALU.mult).then_inc(pr_ok, 1)

            def retention(p):
                for k in range(KD):
                    dve.wait_ge(high1_ok, 2 * p + k + 1)
                    dve.tensor_tensor(xT_parts[1][:, k, :], bank[k], xT_parts[0][:, k, :].bitcast(F32),
                                      ALU.subtract).then_inc(low1_ok, 1)
                if p == 0:
                    for g in range(KD):
                        dve.wait_ge(gram_ok, g + 1)
                        dve.tensor_tensor(gram_parts[1][:, g, :], bank[4 + g][:, 0:D], gram_parts[0][:, g, :].bitcast(F32),
                                          ALU.subtract).then_inc(gram_low_ok, 1)
                if p >= 1:
                    residual1(p - 1)
                if p + 1 < PAIRS:
                    stats1(p + 1)
                dve.wait_ge(u_pe, 2 * p + 2)
                dve.tensor_copy(uT[:, 1, :], bank[1]).then_inc(u_dve, 1)
                if p + 1 < PAIRS:
                    apply1(p + 1)
                if p >= 1:
                    stats2(p - 1)
                dve.wait_ge(v_pe, 2 * p + 2)
                dve.tensor_copy(v1[:, 2:4, :].rearrange("p t d -> p (t d)"), bank[5]).then_inc(v_dve, 1)
                decayed(p)
                if 1 <= p <= 2:
                    for i in range(TPP):
                        apply2(p - 1, i)

            def split(p, which, g):
                dve.wait_ge(rest_ok, (2 * p + which) * G + g + 1)
                link(dve.tensor_copy(parts[:, which, g, 1, :], qk[:, g, :]))
                dve.tensor_tensor(parts[:, which, g, 2, :], qk[:, g, :], parts[:, which, g, 1, :], ALU.subtract
                                  ).then_inc(split_ok, 1)

            def project(p, i):
                if i >= 8:
                    dve.wait_ge(pj_pe, 10 * p + i + 1)
                    if i == 8:
                        dve.wait_ge(ones_ok, 4)
                        if p >= 2:
                            dve.wait_ge(pv_pe, NU * 2 * (p - 1))
                    for j in range(2):
                        dve.tensor_tensor(
                            va[:, p % 2, 2 * (i - 8) + j, :, 0:DH],
                            piece_bank(p, i)[:, j * D:(j + 1) * D].rearrange("p (h w) -> p h w", h=H),
                            bv_s[:].rearrange("p (h w) -> p h w", h=H), ALU.add).then_inc(pj_dve, 1)

            def split_piece(p, i):
                if 5 <= i <= 8:
                    split(p, (i - 5) // 2, (i - 5) % 2)

            def maxima(b, u, j):
                n = 3 * (NU * b + u) + j
                dve.wait_ge(s_pe, n + 1)
                if u == 0 and j == 0 and b >= 2:
                    dve.wait_ge(m_pe, b - 1)
                if j == 0:
                    dve.tensor_reduce(mx[:, b % 2, 0, U * u:U * u + U],
                                      SCORE_BANK[n % 3].rearrange("p (h k) -> p h k", h=U), AX, ALU.max).then_inc(s_max, 1)
                else:
                    h = U * u + 2 * (j - 1)
                    dve.tensor_reduce(mx[:, b % 2, 1, h:h + 2],
                                      SCORE_BANK[n % 3].rearrange("p (h k) -> p h k", h=2), AX, ALU.max).then_inc(s_max, 1)

            def maxima_rows(b):
                dve.wait_ge(m_pe, b + 1)
                if b >= 1:
                    dve.wait_ge(max_in[(b - 1) % 2], 32 * ((b - 1) // 2 + 1))
                link(dve.tensor_scalar(mrow[:, 0, :], bank[7][0:H, 0:S], -1.0, None, ALU.mult))
                dve.scalar_tensor_tensor(out=mrow[:, 1, :], in0=bank[7][0:H, 0:S], scalar=-1.0, in1=mrow[:, 0, :],
                                         op0=ALU.mult, op1=ALU.subtract).then_inc(m_ok, 1)

            def visit(b, v):
                r = b % 2
                if v in (0, SECOND):
                    q = int(v == SECOND)
                    dve.wait_ge(e1_pe, 2 * b + q + 1)
                    heads = bank[5].rearrange("p (h w) -> p h w", w=VW)
                    link(dve.reciprocal(rden[:, q, :].rearrange("p (h a) -> p h a", a=1), heads[:, :, DH:DH + 1]))
                    dve.tensor_tensor(o_n[:, q, :].rearrange("p (h w) -> p h w", w=DH), heads[:, :, 0:DH],
                                      rden[:, q, :].rearrange("p (h a) -> p h a", a=1).to_broadcast((P, H, DH)),
                                      ALU.mult).then_inc(on_ok, 1)
                if v == 2:
                    dve.wait_ge(e3_pe, b + 1)
                    if b >= 2:
                        dve.wait_ge(row_out[r], 16 * (b // 2))
                        dve.wait_ge(scattered[r], 32 * (b // 2))
                    dve.wait_ge(xb_ok, 2 * b + 2)
                    link(dve.tensor_tensor(rec[:, r, :, 0:D], pair[:, :, 0:D], xs[:, 2 * b:2 * b + 2, :], ALU.add))
                    for q in range(2):
                        dve.bn_stats(st3[:, q, :], rec[:, r, q, 0:D]).then_inc(dve_c, 1)
                    chain[0] += 2
                    dve.wait_ge(dve_c, chain[0])
                    dve.bn_aggr(rec[:, r, 0, D:D + 2], st3[:, 0, :])
                    dve.bn_aggr(rec[:, r, 1, D:D + 2], st3[:, 1, :]).then_inc(x3_ok, 1)
                if v == APPLY:
                    dve.wait_ge(rstd3, b + 1)
                    for q in range(2):
                        last = dve.tensor_scalar(x3n[:, q, :], rec[:, r, q, 0:D], rec[:, r, q, D:D + 1],
                                                 rec[:, r, q, D + 1:D + 2], ALU.subtract, ALU.mult)
                    last.then_inc(x3n_ok, 1)
                    dve.tensor_copy(rec[:, r, :, D + 3:REC].bitcast(U32),
                                    cst[:, C_TOK + 2 * b:C_TOK + 2 * b + 2].rearrange("p (q a) -> p q a", a=1))
                if v == 4:
                    dve.wait_ge(e5_pe, b + 1)
                    for q in range(2):
                        dve.max(top[:, q, :], pair[:, q, 0:E]).then_inc(dve_c, 1)
                    chain[0] += 2
                    dve.wait_ge(dve_c, chain[0])
                    for q in range(2):
                        dve.max_index(topi[:, q, :], top[:, q, :], pair[:, q, 0:E]).then_inc(dve_c, 1)
                    chain[0] += 2
                    dve.tensor_scalar(gsm[:, 1, :], top[:, :, 0], -1.0, None, ALU.mult)
                    dve.wait_ge(dve_c, chain[0])
                    link(dve.tensor_copy(gsm[:, 0, :], topi[:, :, 0]))
                    dve.tensor_tensor(hot[:], iota_e.rearrange("p (a e) -> p a e", a=1).to_broadcast((P, 2, E)),
                                      gsm[:, 0, :].rearrange("p (q a) -> p q a", a=1).to_broadcast((P, 2, E)),
                                      ALU.is_equal).then_inc(hot_ok, 1)
                if v == 5:
                    dve.wait_ge(e6_pe, b + 1)
                    dve.wait_ge(gexp_ok, 2 * b + 2)
                    dve.wait_ge(hot_ok, b + 1)
                    dve.reciprocal(rec[:, r, :, D + 2:D + 3], gsm[:, 2, :].rearrange("p (q a) -> p q a", a=1))
                    link(dve.tensor_tensor(ahead[:], pair[:, :, 32:32 + E], hot[:], ALU.mult))
                    link(dve.tensor_reduce(gsm[:, 3, :], ahead[:], AX, ALU.add))
                    dve.tensor_scalar(gsm[:, 4, :], gsm[:, 3, :], float(CAP), FAR, ALU.is_ge, ALU.mult)
                    link(dve.scalar_tensor_tensor(out=gsm[:, 5, :], in0=gsm[:, 0, :], scalar=float(CAP),
                                                  in1=gsm[:, 3, :], op0=ALU.mult, op1=ALU.add))
                    dve.tensor_tensor(slot_u[:, 2 * b:2 * b + 2], gsm[:, 4, :], gsm[:, 5, :], ALU.add
                                      ).then_inc(slot_ok, 1)
                    if b + 1 < B:
                        if b == 0:
                            dve.wait_ge(ones_ok, 2)
                        link(dve.tensor_tensor(ahead[:, 0, :], hot[:, 0, :], hot[:, 1, :], ALU.add))
                        dve.tensor_tensor(seen[:, (b + 1) % 2, :], seen[:, b % 2, :], ahead[:, 0, :], ALU.add
                                          ).then_inc(seen_ok, 1)

            for p in range(PAIRS):
                retention(p)
                if p == FIRST_PROJECTED:
                    for i in range(10):
                        split_piece(0, i)
                        project(0, i)
            for T in range(EARLY):
                maxima(0, T // 3, T % 3)
            residual1(PAIRS - 1)
            for T in STEPS:
                if scored_at(T) and T >= EARLY:
                    b, k = scored_at(T)
                    maxima(b, k // 3, k % 3)
                if T == STATS_AT:
                    stats2(PAIRS - 1)
                if turned_at(T) is not None:
                    maxima_rows(turned_at(T))
                for b, v in visits_at(T, DVE_VISITS):
                    visit(b, v)
                if rows_at(T):
                    apply2(*rows_at(T))
                if piece_at(T):
                    project(*piece_at(T))
                if piece_at(T):
                    split_piece(*piece_at(T))

            def normalise(e):
                dve.wait_ge(xd_in[e % 3], 16 * (e // 3 + 1))
                if e >= 1:
                    dve.wait_ge(xdT_pe, e)
                for j in range(2):
                    last = dve.tensor_scalar(xdn[:, j, :], xd[:, e % 3, j, 0:D], xd[:, e % 3, j, D:D + 1],
                                             xd[:, e % 3, j, D + 1:D + 2], ALU.subtract, ALU.mult)
                last.then_inc(xdn_ok, 1)

            def finish(e):
                dve.wait_ge(z_pe, e + 1)
                if e >= 2:
                    dve.wait_ge(final_out[e % 2], 32 * (e // 2))
                for j in range(2):
                    last = dve.scalar_tensor_tensor(
                        out=yo[:, e % 2, j, :], in0=bank[5][0:HALF, j * D:(j + 1) * D],
                        scalar=xd[:, e % 3, j, D + 2:D + 3], in1=xd[:, e % 3, j, 0:D], op0=ALU.mult, op1=ALU.add)
                last.then_inc(yo_ok, 1)

            normalise(0)
            for e in range(E):
                if e + 1 < E:
                    normalise(e + 1)
                dve.wait_ge(h_pe, 3 * e + 2)
                dve.tensor_scalar(hT[:, 3:6, :].rearrange("p f c -> p (f c)"), bank[2][:, 0:3 * CAP], 0.0, None,
                                  ALU.max).then_inc(h_dve, 1)
                if e >= 1:
                    finish(e - 1)
            finish(E - 1)

        @block.tensor
        def _(pe):
            def stay_warm(products):
                for _ in range(products):
                    pe.matmul(bank[7][:, 0:P], ones_b[:], ones_b[:], start=True, stop=True)

            pe.wait_ge(ones_ok, 1)
            stay_warm(WARM_START)
            pe.wait_ge(id_in, 16)
            pe.wait_ge(wa_in, 16 * 2)
            for i in range(4):
                w, kc = i // 2, i % 2
                for r in range(KD):
                    last = pe.transpose(bank[4 + i][:, r * P:(r + 1) * P], wqk1[:, w, r, kc * P:(kc + 1) * P], ident)
                last.then_inc(wT_pe, 1)
            pe.wait_ge(wv_in, 16 * 2)
            for k in range(KD):
                last = pe.transpose(bank[2][:, k * E:(k + 1) * E], gw_s[:, k * P:(k + 1) * P], ident[0:E, 0:E])
            last.then_inc(wT_pe, 1)
            def turn_rows(p):
                pe.wait_ge(xn1_ok, p + 1)
                for k in range(KD):
                    for i in range(TPP):
                        last = pe.transpose(bank[k][:, i * P:(i + 1) * P], xn1[:, i, k * P:(k + 1) * P], ident)
                    last.then_inc(t1_pe, 1)

            def fold_weights():
                pe.wait_ge(wT_ok, 4)
                for m in range(KD):
                    for k in range(KD):
                        last = pe.matmul(bank[4 + m][:, 0:D], wqk1T[:, 0, k, m * P:(m + 1) * P], wqk1T[:, 1, k, :],
                                         start=(k == 0), stop=(k == KD - 1))
                    last.then_inc(gram_pe, 1)

            def fold(p):
                pe.wait_ge(low1_ok, 2 * (p + 1))
                if p == 0:
                    pe.wait_ge(gram_low_ok, KD)
                    pe.wait_ge(wT_ok, 5)
                for m in range(KD):
                    for k in range(KD):
                        for a, b in PASSES:
                            last = pe.matmul(bank[m], gram_parts[a][:, k, m * P:(m + 1) * P], xT_parts[b][:, k, :],
                                             start=(k == 0 and a == b), stop=(k == KD - 1 and b == 1))
                    last.then_inc(u_pe, 1)

            def values1(p):
                if p == 0:
                    pe.wait_ge(wv1_low_ok, 1)
                for i in range(TPP):
                    for k in range(KD):
                        for a, b in PASSES:
                            last = pe.matmul(bank[4 + i // 2][:, (i % 2) * D:(i % 2 + 1) * D],
                                             xT_parts[a][:, k, i * P:(i + 1) * P], wv1_parts[b][:, k, :],
                                             start=(k == 0 and a == b), stop=(k == KD - 1 and b == 1),
                                             skip_group_check=True)
                    if i % 2:
                        last.then_inc(v_pe, 1)

            def scores1(p):
                pe.wait_ge(whole1_ok, 2 * (p + 1))
                pe.wait_ge(u_act, p + 1)
                pe.wait_ge(u_dve, p + 1)
                for i in range(2):
                    o = i * S
                    for k in range(KD):
                        pe.matmul(bank[6 + i][:, 0:S], xT[:, k, o:o + P], uT[:, k, o:o + S],
                                  start=(k == 0), stop=(k == KD - 1))
                    for k in range(KD):
                        last = pe.matmul(bank[6 + i][:, S:S + P], xT[:, k, o + P:o + S], uT[:, k, o + P:o + S],
                                         start=(k == 0), stop=(k == KD - 1))
                    last.then_inc(s1_pe, 1)

            def retain(p):
                if p >= 1:
                    pe.wait_ge(x1_ok, TPP * p)
                if p == FIRST_PROJECTED:
                    pe.wait_ge(pj_dve, 4)
                pe.wait_ge(pr_ok, 4 * (p + 1))
                pe.wait_ge(v_act, p + 1)
                pe.wait_ge(v_dve, p + 1)
                for i in range(TPP):
                    b, q = i // 2, i % 2
                    dst = bank[2 + i // 2][:, q * D:(q + 1) * D]
                    last = pe.matmul(dst, pr[:, b, q * P:(q + 1) * P], v1[:, 2 * b, :], start=True, stop=(q == 0))
                    if q == 1:
                        last = pe.matmul(dst, pr[:, b, 2 * P:3 * P], v1[:, 2 * b + 1, :], start=False, stop=True)
                    last.then_inc(o1_pe, 1)

            turned = [0]

            def pieces_read(p, i):
                p, i = (p, i) if i else (p - 1, 10)
                if i <= 8:
                    pe.wait_ge(pj_act, 8 * p + i)
                else:
                    pe.wait_ge(pj_dve, 4 * p + 2 * (i - 8))

            def project(p, i):
                if p >= 1:
                    pieces_read(p, i)
                    if turned[0]:
                        pe.wait_ge(m_ok, turned[0])
                elif i >= 2:
                    pe.wait_ge(pj_act, i - 1)
                if i in (4, 6):
                    pe.wait_ge(pj_act, 8 * p + i - 2)
                if i < 4:
                    k = i % 2
                    if i == 0:
                        pe.wait_ge(xn2_ok, TPP * (p + 1))
                    if i == 2:
                        pe.wait_ge(c_in[p], 16)
                    for t in range(TPP):
                        src = (xn2[:, p % 2, t, k * P:(k + 1) * P] if i < 2 else cx[:, t, k * P:(k + 1) * P])
                        last = pe.transpose(piece_bank(p, i)[:, t * P:(t + 1) * P], src, ident)
                elif i < 8:
                    which, g = (i - 4) // 2, i % 2
                    for k in range(KD):
                        last = pe.matmul(piece_bank(p, i), (wq_p, wk_p)[which][:, k, g].rearrange("p d h -> p (d h)"),
                                         (xT, cT)[which][:, k, :], start=(k == 0), stop=(k == KD - 1))
                else:
                    for j in range(2):
                        t = 2 * (i - 8) + j
                        for k in range(KD):
                            last = pe.matmul(piece_bank(p, i)[:, j * D:(j + 1) * D], cT[:, k, t * P:(t + 1) * P],
                                             wv_s[:, k, :], start=(k == 0), stop=(k == KD - 1), skip_group_check=True)
                last.then_inc(pj_pe, 1)

            def scores(b, u, j):
                n = 3 * (NU * b + u) + j
                p, o, dst = b // 2, (b % 2) * S, SCORE_BANK[n % 3]
                if n >= 3:
                    pe.wait_ge(s_max, n - 2)
                if n % (6 * NU) == 0:
                    pe.wait_ge(stack_in[p], STACKED)
                if j == 0:
                    pe.matmul(dst, ident_b[:], mask_b[:], start=True, stop=False, skip_group_check=True)
                    for i in range(U):
                        h = U * u + i
                        last = pe.matmul(dst[:, i * P:(i + 1) * P], qst[0:KS, p % 2, h, o:o + P],
                                         kst[0:KS, p % 2, h, o:o + P], start=False, stop=(i == U - 1),
                                         skip_group_check=True)
                else:
                    pe.matmul(dst.rearrange("p (h k) -> p h k", h=2)[:, :, P:S], ident_b[:],
                              mask_b[:, 0:S].rearrange("p (h k) -> p h k", h=2), start=True, stop=False,
                              skip_group_check=True)
                    for i in range(2):
                        h = U * u + 2 * (j - 1) + i
                        last = pe.matmul(dst[:, i * S:(i + 1) * S], qst[0:KS, p % 2, h, o + P:o + S],
                                         kst[0:KS, p % 2, h, o:o + S], start=False, stop=(i == 1),
                                         skip_group_check=True)
                last.then_inc(s_pe, 1)

            def maxima_turned(b, T):
                pe.wait_ge(s_max, 3 * NU * (b + 1))
                pieces_read(*next_piece(T))
                if b >= 1:
                    pe.wait_ge(m_ok, b)
                for q in range(2):
                    last = pe.transpose(bank[7][0:H, q * P:(q + 1) * P], mx[:, b % 2, q, :], ident)
                last.then_inc(m_pe, 1)
                turned[0] = b + 1

            def shifted(b, u, j):
                n = 3 * (NU * b + u) + j
                p, o, dst = b // 2, (b % 2) * S, bank[2 + n % 2]
                if n >= 2:
                    pe.wait_ge(exp_ok, n - 1)
                if n == 0:
                    pe.wait_ge(x1_ok, NT)
                    pe.wait_ge(kone_in, 32)
                if u == 0 and j == 0:
                    pe.wait_ge(max_in[b % 2], 32 * (b // 2 + 1))
                for i in range(U if j == 0 else 2):
                    if j == 0:
                        h = U * u + i
                        last = pe.matmul(dst[:, i * P:(i + 1) * P], kst[:, p % 2, h, o + P:o + S],
                                         qst[:, p % 2, h, o + P:o + S], start=True, stop=True)
                    else:
                        h = U * u + 2 * (j - 1) + i
                        last = pe.matmul(dst[:, i * S:(i + 1) * S], kst[:, p % 2, h, o:o + P],
                                         qst[:, p % 2, h, o:o + S], start=True, stop=True)
                last.then_inc(st_pe, 1)

            def weigh(b, u):
                n = NU * b + u
                pe.wait_ge(sel_ok, 3 * (n + 1))
                if n >= 1:
                    pe.wait_ge(ot_ok, n)
                if u == 0 and b % 2 == 0:
                    pe.wait_ge(pj_dve, 4 * (b // 2 + 1))
                for kt_ in range(2):
                    for i in range(U):
                        lhs = va[:, (b // 2) % 2, 2 * (b % 2) + kt_, U * u + i, :]
                        if kt_ == 0:
                            rhs = pT[:, (3 * n + 1 + i // 2) % 6, (i % 2) * S:(i % 2 + 1) * S]
                            dst = bank[4][VW * i:VW * (i + 1), 0:S]
                        else:
                            rhs = pT[:, (3 * n) % 6, i * P:(i + 1) * P]
                            dst = bank[4][VW * i:VW * (i + 1), P:S]
                        last = pe.matmul(dst, lhs, rhs, start=(kt_ == 0), stop=(kt_ == 1), skip_group_check=True)
                last.then_inc(pv_pe, 1)

            def visit(b, v):
                if v in (0, SECOND):
                    q = int(v == SECOND)
                    if q == 0:
                        pe.wait_ge(ot_ok, NU * (b + 1))
                        if b >= 1:
                            pe.wait_ge(slot_ok, b)
                    else:
                        pe.wait_ge(on_ok, 2 * b + 1)
                    for u in range(NU):
                        last = pe.transpose(bank[5][:, u * P:(u + 1) * P], oT[:, b % 2, u, q * P:(q + 1) * P], ident)
                    last.then_inc(e1_pe, 1)
                if v == 1:
                    pe.wait_ge(on_ok, 2 * b + 2)
                    for q in range(2):
                        for k in range(KD):
                            last = pe.transpose(pair[:, q, k * P:(k + 1) * P], o_n[:, q, k * P:(k + 1) * P], ident)
                    last.then_inc(e2_pe, 1)
                if v == 2:
                    pe.wait_ge(oT2_ok, b + 1)
                    for q in range(2):
                        for k in range(KD):
                            last = pe.matmul(pair[:, q, 0:D], oT2[:, q, k, :], wo_s[:, k, :], start=(k == 0),
                                             stop=(k == KD - 1))
                    last.then_inc(e3_pe, 1)
                if v == 3:
                    pe.wait_ge(x3n_ok, b + 1)
                    for q in range(2):
                        for k in range(KD):
                            last = pe.transpose(pair[:, q, k * P:(k + 1) * P], x3n[:, q, k * P:(k + 1) * P], ident)
                    last.then_inc(e4_pe, 1)
                if v == 4:
                    pe.wait_ge(x3T_ok, b + 1)
                    for q in range(2):
                        for k in range(KD):
                            last = pe.matmul(pair[:, q, 0:E], x3T[:, q, k, :], gwT[:, k, :], start=(k == 0),
                                             stop=(k == KD - 1))
                    last.then_inc(e5_pe, 1)
                if v == 5:
                    pe.wait_ge(hot_ok, b + 1)
                    pe.wait_ge(gexp_ok, 2 * b + 2)
                    if b >= 1:
                        pe.wait_ge(seen_ok, b)
                    for q in range(2):
                        dst = pair[:, q, 32:32 + E]
                        pe.matmul(dst, before_b[:], hot[:, q, :], start=True, stop=False)
                        if q == 1:
                            pe.matmul(dst, ones_b[:], hot[:, 0, :], start=False, stop=False)
                        last = pe.matmul(dst, ones_b[:], seen[:, b % 2, :], start=False, stop=True)
                    last.then_inc(e6_pe, 1)

            for p in range(PAIRS):
                turn_rows(p)
                if p == 0:
                    fold_weights()
                else:
                    retain(p - 1)
                fold(p)
                values1(p)
                scores1(p)
                if p == FIRST_PROJECTED:
                    pe.wait_ge(perm_ok, 2 * KD * G)
                    pe.wait_ge(x1_ok, TPP * FIRST_PROJECTED)
                    for i in range(10):
                        project(0, i)
            pe.wait_ge(cast_ok, 6)
            pe.wait_ge(ones_ok, 4)
            for T in range(EARLY):
                scores(0, T // 3, T % 3)
            retain(PAIRS - 1)
            for T in STEPS:
                if scored_at(T) and T >= EARLY:
                    b, k = scored_at(T)
                    scores(b, k // 3, k % 3)
                if B * BANKS < T < (B + 1) * BANKS + LEAD + PE_VISITS[0]:
                    pe.wait_ge(m_ok, B)
                    stay_warm(WARM_TAIL)
                if weighed_at(T):
                    b, k = weighed_at(T)
                    shifted(b, k // 3, k % 3)
                if piece_at(T):
                    project(*piece_at(T))
                for b, v in visits_at(T, PE_VISITS):
                    if b == B - 1:
                        pe.wait_ge(m_ok, B)
                        stay_warm(WARM_VISITS[v])
                    visit(b, v)
                if turned_at(T) is not None:
                    maxima_turned(turned_at(T), T)
                if sums_at(T) is not None:
                    weigh(*divmod(sums_at(T), NU))

            def turn_slots(e):
                pe.wait_ge(xdn_ok, e + 1)
                for k in range(KD):
                    for j in range(2):
                        last = pe.transpose(bank[0][:, k * CAP + j * HALF:k * CAP + (j + 1) * HALF],
                                            xdn[:, j, k * P:(k + 1) * P], ident[0:HALF, 0:HALF])
                last.then_inc(xdT_pe, 1)

            def hidden(e):
                pe.wait_ge(xdT_ok, e + 1)
                pe.wait_ge(w1_in[e % WR], 16 * (e // WR + 1))
                for f in range(FT):
                    for k in range(KD):
                        last = pe.matmul(bank[1 + f // 3][:, (f % 3) * CAP:(f % 3 + 1) * CAP],
                                         w1_s[e % WR][:, k, f * P:(f + 1) * P], xdT[:, k, :],
                                         start=(k == 0), stop=(k == KD - 1), skip_group_check=True)
                    if f % 3 == 2 or f == FT - 1:
                        last.then_inc(h_pe, 1)

            def back(e):
                pe.wait_ge(yT_ok, e + 1)
                if e >= 1:
                    pe.wait_ge(yo_ok, e)
                for j in range(2):
                    for k in range(KD):
                        last = pe.transpose(bank[5][0:HALF, j * D + k * P:j * D + (k + 1) * P],
                                            yT[:, k, j * HALF:(j + 1) * HALF], ident)
                last.then_inc(z_pe, 1)

            def outward(e):
                pe.wait_ge(w2_in[e % WR], 16 * (e // WR + 1))
                for k in range(KD):
                    for f in range(FT):
                        if k == 0 and f in (0, 6):
                            pe.wait_ge(h_act, 2 * e + 1 + (f == 6))
                        if k == 0 and f == 3:
                            pe.wait_ge(h_dve, e + 1)
                        last = pe.matmul(bank[4][:, k * CAP:(k + 1) * CAP], w2_s[e % WR][:, f, k * P:(k + 1) * P],
                                         hT[:, f, :], start=(f == 0), stop=(f == FT - 1), skip_group_check=True)
                last.then_inc(y_pe, 1)

            stay_warm(WARM_SLOTS)
            turn_slots(0)
            for e in range(E):
                hidden(e)
                if e >= 1:
                    back(e - 1)
                if e + 1 < E:
                    turn_slots(e + 1)
                outward(e)
            back(E - 1)


BANKS = 3 * NU
LAST = BANKS - 1
LEAD = 3
FIRST_PROJECTED = PAIRS - 2
NORM, APPLY, SECOND = 6, 7, 8
PE_VISITS = {0: 4, SECOND: 5, 1: 6, 2: 8, 3: 12, 4: 13, 5: 15}
DVE_VISITS = {0: 4, SECOND: 5, 2: 8, APPLY: 9, 4: 13, 5: 15}
ACT_VISITS = {1: 6, 3: 11, 4: 14}
POOL_VISITS = {NORM: 9, 5: 18}
SP_VISITS = {3: 12}
PIECES = (2, 4, 6, 8, 11, 13, 15, 18, 20, 22)
NEXT_ROWS = (12, 13, 14, 15)
EARLY, STATS_AT = 2, 7
WARM_START = 60
WARM_VISITS = {0: 15, SECOND: 20, 1: 15, 2: 15, 3: 35, 4: 15, 5: 15}
WARM_TAIL = 5
WARM_SLOTS = 120
STEPS = range((B + 1) * BANKS + LEAD + max(POOL_VISITS.values()) + 1)


def scored_at(T):
    return divmod(T, BANKS) if T < B * BANKS else None


def weighed_at(T):
    t = T - BANKS - LEAD
    return divmod(t, BANKS) if 0 <= t < B * BANKS else None


def sums_at(T):
    t = T - BANKS - LEAD
    return t // 3 - 1 if t % 3 == 2 and 3 <= t < B * BANKS + 3 else None


def visits_at(T, visits):
    return [(b, v) for b in range(B) for v, late in visits.items() if T == (b + 2) * BANKS + LEAD + late]


def piece_at(T):
    p, r = divmod(T + 2 * BANKS, 2 * BANKS)
    return (p, PIECES.index(r)) if 1 <= p < PAIRS and r in PIECES else None


def rows_at(T):
    p, r = divmod(T, 2 * BANKS)
    return (p + 2, NEXT_ROWS.index(r)) if 0 <= p < PAIRS - 2 and r in NEXT_ROWS else None


def next_piece(T):
    later = [piece_at(t) for t in range(T + 1, T + 1 + 2 * BANKS) if piece_at(t)]
    return later[0] if later else (PAIRS, 0)


def turned_at(T):
    t = T
    return t // BANKS if t % BANKS == LAST and 0 <= t < B * BANKS else None


_INS = ['x', 'ctx_1024', 'L0_attn_weight_q', 'L0_attn_weight_k', 'L0_attn_weight_v', 'L0_attn_theta',
        'L0_xattn_wq', 'L0_xattn_bq', 'L0_xattn_wk', 'L0_xattn_bk', 'L0_xattn_wv', 'L0_xattn_bv',
        'L0_xattn_wo', 'L0_xattn_bo', 'L0_ffn_gate_w', 'L0_ffn_w1', 'L0_ffn_w2']


def constants():
    import numpy as np
    r, c = np.arange(P)[:, None], np.arange(P)[None, :]
    q = np.arange(2 * P)[None, :]
    decay = np.where(q >= r, np.float32(0.96875) ** np.maximum(q - r, 0).astype(np.float32), 0)
    return np.concatenate([
        np.eye(P), decay, np.where(c > r, NEG, 0), (r < c), np.broadcast_to(np.arange(E)[None, :], (P, E)),
        r + P * np.arange(NT)[None, :]], axis=1).astype(np.float32)


def kernel(**inputs):
    import numpy as _np
    import concourse.bacc as _bacc
    from concourse import mybir as _mybir
    from concourse.bass_utils import run_bass_kernel_spmd as _run

    nc = _bacc.Bacc("TRN2", target_bir_lowering=False, num_devices=1)
    arrays, args = {}, []
    for name, a in [(n, inputs[n]) for n in _INS] + [("constants", constants())]:
        a = _np.ascontiguousarray(a)
        arrays[f"in_{name}_dram"] = a
        args.append(nc.dram_tensor(f"in_{name}_dram", a.shape, _mybir.dt.from_np(a.dtype), kind="ExternalInput").ap())
    out = nc.dram_tensor("out_0_dram", (B, S, D), _mybir.dt.float32, kind="ExternalOutput").ap()
    decoder_layer(nc, *args, out)
    r = _run(nc, [arrays], core_ids=[0])
    return r.results[0]["out_0_dram"]
```
